# Optimizing a Trainium2 kernel written in Bass

```python
import numpy as np
import jax
import jax.numpy as jnp

def _softmax(x, axis=-1):
    return jax.nn.softmax(x, axis=axis)

def _gelu(x):
    return jax.nn.gelu(x, approximate=True)

def _silu(x):
    return jax.nn.silu(x)

def _sigmoid(x):
    return jax.nn.sigmoid(x)

def _layernorm(x, axis=-1, eps=1e-05):
    m = jnp.mean(x, axis=axis, keepdims=True)
    v = jnp.var(x, axis=axis, keepdims=True)
    return (x - m) / jnp.sqrt(v + eps)

def _scatter_add(tgt, idx, src, axis=0):
    return tgt.at[idx].add(src)

def _segment_sum(src, seg, n):
    return jax.ops.segment_sum(src, seg, n)
kernel_name = 'mk_xattn_ffn_d2_seqx_r4_003c7b'

def setup_inputs(seed: int=0):
    np.random.seed(seed)
    _w = jnp.asarray

    def _rec_inputs():
        import jax
        import jax.numpy as jnp
        _rk = jax.random.key(seed)
        x = -0.0002928 + 1 * jax.random.normal(jax.random.fold_in(_rk, 1), (16, 112, 256), jnp.float32)
        _lenS = 112 - jax.random.randint(jax.random.fold_in(_rk, 7), (16,), 0, max(1, 112 // 4) + 1, jnp.int32)
        _lenS2 = 375 - jax.random.randint(jax.random.fold_in(_rk, 8), (16,), 0, max(1, 375 // 4) + 1, jnp.int32)
        _ctx_512P = jax.random.normal(jax.random.fold_in(_rk, 11), (16, 16, 128), jnp.float32)
        _ctx_512c = jax.random.dirichlet(jax.random.fold_in(_rk, 511), 0.3 * jnp.ones((16,), jnp.float32), (16, 375))
        _ctx_512t = jnp.einsum('bsk,bkd->bsd', _ctx_512c, _ctx_512P)
        _ctx_512t = _ctx_512t * jax.lax.rsqrt(jnp.mean(jnp.square(_ctx_512t)) + 1e-12) * 0.953939
        ctx_512 = -0.000514642 + 1.00011 * (_ctx_512t + 0.3 * jax.random.normal(jax.random.fold_in(_rk, 611), (16, 375, 128), jnp.float32))
        return (x, ctx_512)
    x, ctx_512 = _rec_inputs()

    def _L0_xattn_setup():
        import jax, jax.numpy as jnp
        import numpy as np
        DIM = 256
        LATENT_DIM = 128
        NUM_HEADS = 16
        HEAD_DIM = DIM // NUM_HEADS
        SCALE = HEAD_DIM ** (-0.5)
        key = jax.random.key(seed)
        k1, k2, k3, k4, k5 = jax.random.split(key, 5)
        B, xN, zN = (2, 512, 512)
        x = jax.random.normal(k1, (B, xN, DIM), dtype=jnp.float32)
        z = jax.random.normal(k2, (B, zN, LATENT_DIM), dtype=jnp.float32)
        Wq = jax.random.normal(k3, (DIM, DIM), dtype=jnp.float32) * DIM ** (-0.5)
        Wkv = jax.random.normal(k4, (2 * DIM, LATENT_DIM), dtype=jnp.float32) * LATENT_DIM ** (-0.5)
        Wo = jax.random.normal(k5, (DIM, DIM), dtype=jnp.float32) * DIM ** (-0.5)
        return {'x': x, 'z': z, 'Wq': Wq, 'Wkv': Wkv, 'Wo': Wo}
    _L0_xattn_all = _L0_xattn_setup()
    _L0_xattn_in = {k: v for k, v in _L0_xattn_all.items() if k in ('Wq', 'Wkv', 'Wo')}
    del _L0_xattn_all

    def _L0_ffn_setup():
        import jax, jax.numpy as jnp
        import numpy as np
        S, B, H, F, E, K = (512, 2, 256, 512, 8, 2)

        def _moe_forward(hidden_states, router_w, w1, b1, w2, b2):
            s, b, h = hidden_states.shape
            T = s * b
            x = hidden_states.reshape(T, h)
            logits = jnp.einsum('th,eh->te', x, router_w)
            topk_logits, topk_idx = jax.lax.top_k(logits, K)
            probs = jax.nn.softmax(topk_logits, axis=-1)
            combine = jnp.zeros((T, E), dtype=x.dtype)
            combine = combine.at[jnp.arange(T)[:, None], topk_idx].add(probs.astype(x.dtype))
            hmid = jnp.einsum('th,efh->etf', x, w1) + b1[:, None, :]
            hmid = jax.nn.gelu(hmid, approximate=False)
            y = jnp.einsum('etf,ehf->eth', hmid, w2) + b2[:, None, :]
            out = jnp.einsum('eth,te->th', y, combine)
            return out.reshape(s, b, h)
        key = jax.random.key(seed)
        ks = jax.random.split(key, 6)
        std = 0.02
        return {'hidden_states': jax.random.normal(ks[0], (S, B, H), dtype=jnp.float32), 'router_w': jax.random.normal(ks[1], (E, H), dtype=jnp.float32) * std, 'w1': jax.random.normal(ks[2], (E, F, H), dtype=jnp.float32) * (1.0 / np.sqrt(H)), 'b1': jnp.zeros((E, F), dtype=jnp.float32), 'w2': jax.random.normal(ks[3], (E, H, F), dtype=jnp.float32) * (1.0 / np.sqrt(F)), 'b2': jnp.zeros((E, H), dtype=jnp.float32)}
    _L0_ffn_all = _L0_ffn_setup()
    _L0_ffn_in = {k: v for k, v in _L0_ffn_all.items() if k in ('router_w', 'w1', 'b1', 'w2', 'b2')}
    del _L0_ffn_all

    def _L1_xattn_setup():
        import jax, jax.numpy as jnp
        import numpy as np
        H, D, C1, C2, S, M, B, W = (16, 32, 256, 128, 512, 128, 2, 4)

        def _ln(x, g, b):
            m = jnp.mean(x, -1, keepdims=True)
            v = jnp.var(x, -1, keepdims=True)
            return (x - m) * jax.lax.rsqrt(v + 1e-05) * g + b

        def _mha(x, y, wq, wk, wv, li1_w, li1_b, lnx_g, lnx_b, lny_g, lny_b, ln3_g, ln3_b, li2_w, li2_b, li3_w, li3_b, causal):
            xn = _ln(x, lnx_g, lnx_b)
            yn = _ln(y, lny_g, lny_b)
            q = jnp.einsum('bsc,hcd->bhsd', xn, wq)
            k = jnp.einsum('btc,hcd->bhtd', yn, wk)
            v = jnp.einsum('btc,hcd->bhtd', yn, wv)
            a = jax.nn.softmax(jnp.einsum('bhsd,bhtd->bhst', q, k) * D ** (-0.5), axis=-1)
            if causal:
                s, t = (a.shape[-2], a.shape[-1])
                mask = (jnp.arange(t)[None, :] > jnp.arange(s)[:, None]).astype(a.dtype)
                a = a * mask
            o = jnp.einsum('bhst,bhtd->bhsd', a, v)
            o = o.transpose(0, 2, 1, 3).reshape(x.shape[0], x.shape[1], H * D)
            x_out = x + o @ li1_w + li1_b
            h = jax.nn.gelu(_ln(x_out, ln3_g, ln3_b) @ li2_w + li2_b, approximate=False)
            return x_out + h @ li3_w + li3_b
        key = jax.random.key(seed)
        ks = iter(jax.random.split(key, 64))

        def w(shape, scale=0.02):
            return jax.random.normal(next(ks), shape, jnp.float32) * scale
        inp = {'xx': jax.random.normal(next(ks), (B, S, C1), jnp.float32), 'ee': jax.random.normal(next(ks), (B, M, C2), jnp.float32), 'ln1_g': jnp.ones(C1, jnp.float32), 'ln1_b': jnp.zeros(C1, jnp.float32), 'ln2_g': jnp.ones(C1, jnp.float32), 'ln2_b': jnp.zeros(C1, jnp.float32)}
        for pfx, cy in (('a1', C1), ('a2', C2)):
            inp[pfx + '_wq'] = w((H, C1, D))
            inp[pfx + '_wk'] = w((H, cy, D))
            inp[pfx + '_wv'] = w((H, cy, D))
            inp[pfx + '_li1_w'] = w((H * D, C1))
            inp[pfx + '_li1_b'] = jnp.zeros(C1, jnp.float32)
            inp[pfx + '_lnx_g'] = jnp.ones(C1, jnp.float32)
            inp[pfx + '_lnx_b'] = jnp.zeros(C1, jnp.float32)
            inp[pfx + '_lny_g'] = jnp.ones(cy, jnp.float32)
            inp[pfx + '_lny_b'] = jnp.zeros(cy, jnp.float32)
            inp[pfx + '_ln3_g'] = jnp.ones(C1, jnp.float32)
            inp[pfx + '_ln3_b'] = jnp.zeros(C1, jnp.float32)
            inp[pfx + '_li2_w'] = w((C1, C1 * W))
            inp[pfx + '_li2_b'] = jnp.zeros(C1 * W, jnp.float32)
            inp[pfx + '_li3_w'] = w((C1 * W, C1))
            inp[pfx + '_li3_b'] = jnp.zeros(C1, jnp.float32)
        inp['training'] = 0
        return inp
    _L1_xattn_all = _L1_xattn_setup()
    _L1_xattn_in = {k: v for k, v in _L1_xattn_all.items() if k in ('ln1_g', 'ln1_b', 'ln2_g', 'ln2_b', 'a1_wq', 'a1_wk', 'a1_wv', 'a1_li1_w', 'a1_li1_b', 'a1_lnx_g', 'a1_lnx_b', 'a1_lny_g', 'a1_lny_b', 'a1_ln3_g', 'a1_ln3_b', 'a1_li2_w', 'a1_li2_b', 'a1_li3_w', 'a1_li3_b', 'a2_wq', 'a2_wk', 'a2_wv', 'a2_li1_w', 'a2_li1_b', 'a2_lnx_g', 'a2_lnx_b', 'a2_lny_g', 'a2_lny_b', 'a2_ln3_g', 'a2_ln3_b', 'a2_li2_w', 'a2_li2_b', 'a2_li3_w', 'a2_li3_b')}
    del _L1_xattn_all

    def _L1_ffn_setup():
        import jax, jax.numpy as jnp
        import numpy as np
        B, T, D = (1, 512, 256)
        E, DFF = (8, 1024)

        def _gating(logits):
            S, num_e = logits.shape
            gates = jax.nn.softmax(logits.astype(jnp.float32), axis=1)
            idx1 = jnp.argmax(gates, axis=1)
            mask1 = jax.nn.one_hot(idx1, num_e, dtype=jnp.int32)
            logits_ex1 = jnp.where(mask1.astype(bool), -jnp.inf, logits)
            idx2 = jnp.argmax(logits_ex1, axis=1)
            mask2 = jax.nn.one_hot(idx2, num_e, dtype=jnp.int32)
            loc1 = jnp.cumsum(mask1, axis=0) - 1
            loc2 = jnp.cumsum(mask2, axis=0) - 1 + jnp.sum(mask1, axis=0, keepdims=True)
            loc1_s = jnp.sum(loc1 * mask1, axis=1)
            loc2_s = jnp.sum(loc2 * mask2, axis=1)
            g1 = jnp.sum(gates * mask1, axis=1)
            g2 = jnp.sum(gates * mask2, axis=1)
            denom = jnp.maximum(g1 + g2, jnp.finfo(jnp.float32).eps)
            g1, g2 = (g1 / denom, g2 / denom)
            cap = S
            loc1_sc = jax.nn.one_hot(loc1_s, cap, dtype=jnp.float32)
            loc2_sc = jax.nn.one_hot(loc2_s, cap, dtype=jnp.float32)
            combine = (g1[:, None] * mask1)[:, :, None] * loc1_sc[:, None, :] + (g2[:, None] * mask2)[:, :, None] * loc2_sc[:, None, :]
            dispatch_mask = combine != 0
            return (combine.astype(logits.dtype), dispatch_mask)
        key = jax.random.key(seed)
        k1, k2, k3, k4 = jax.random.split(key, 4)
        x = jax.random.normal(k1, (B, T, D), dtype=jnp.float32)
        Wg = jax.random.normal(k2, (D, E), dtype=jnp.float32) * (1.0 / np.sqrt(D))
        w1 = jax.random.normal(k3, (D, DFF), dtype=jnp.float32) * (1.0 / np.sqrt(D))
        w2 = jax.random.normal(k4, (DFF, D), dtype=jnp.float32) * (1.0 / np.sqrt(DFF))
        return {'x': x, 'Wg': Wg, 'w1': w1, 'w2': w2}
    _L1_ffn_all = _L1_ffn_setup()
    _L1_ffn_in = {k: v for k, v in _L1_ffn_all.items() if k in ('Wg', 'w1', 'w2')}
    del _L1_ffn_all
    return {'x': x, 'ctx_512': ctx_512, 'L0_xattn_Wq': _L0_xattn_in['Wq'], 'L0_xattn_Wkv': _L0_xattn_in['Wkv'], 'L0_xattn_Wo': _L0_xattn_in['Wo'], 'L0_ffn_router_w': _L0_ffn_in['router_w'], 'L0_ffn_w1': _L0_ffn_in['w1'], 'L0_ffn_b1': _L0_ffn_in['b1'], 'L0_ffn_w2': _L0_ffn_in['w2'], 'L0_ffn_b2': _L0_ffn_in['b2'], 'L1_xattn_ln1_g': _L1_xattn_in['ln1_g'], 'L1_xattn_ln1_b': _L1_xattn_in['ln1_b'], 'L1_xattn_ln2_g': _L1_xattn_in['ln2_g'], 'L1_xattn_ln2_b': _L1_xattn_in['ln2_b'], 'L1_xattn_a1_wq': _L1_xattn_in['a1_wq'], 'L1_xattn_a1_wk': _L1_xattn_in['a1_wk'], 'L1_xattn_a1_wv': _L1_xattn_in['a1_wv'], 'L1_xattn_a1_li1_w': _L1_xattn_in['a1_li1_w'], 'L1_xattn_a1_li1_b': _L1_xattn_in['a1_li1_b'], 'L1_xattn_a1_lnx_g': _L1_xattn_in['a1_lnx_g'], 'L1_xattn_a1_lnx_b': _L1_xattn_in['a1_lnx_b'], 'L1_xattn_a1_lny_g': _L1_xattn_in['a1_lny_g'], 'L1_xattn_a1_lny_b': _L1_xattn_in['a1_lny_b'], 'L1_xattn_a1_ln3_g': _L1_xattn_in['a1_ln3_g'], 'L1_xattn_a1_ln3_b': _L1_xattn_in['a1_ln3_b'], 'L1_xattn_a1_li2_w': _L1_xattn_in['a1_li2_w'], 'L1_xattn_a1_li2_b': _L1_xattn_in['a1_li2_b'], 'L1_xattn_a1_li3_w': _L1_xattn_in['a1_li3_w'], 'L1_xattn_a1_li3_b': _L1_xattn_in['a1_li3_b'], 'L1_xattn_a2_wq': _L1_xattn_in['a2_wq'], 'L1_xattn_a2_wk': _L1_xattn_in['a2_wk'], 'L1_xattn_a2_wv': _L1_xattn_in['a2_wv'], 'L1_xattn_a2_li1_w': _L1_xattn_in['a2_li1_w'], 'L1_xattn_a2_li1_b': _L1_xattn_in['a2_li1_b'], 'L1_xattn_a2_lnx_g': _L1_xattn_in['a2_lnx_g'], 'L1_xattn_a2_lnx_b': _L1_xattn_in['a2_lnx_b'], 'L1_xattn_a2_lny_g': _L1_xattn_in['a2_lny_g'], 'L1_xattn_a2_lny_b': _L1_xattn_in['a2_lny_b'], 'L1_xattn_a2_ln3_g': _L1_xattn_in['a2_ln3_g'], 'L1_xattn_a2_ln3_b': _L1_xattn_in['a2_ln3_b'], 'L1_xattn_a2_li2_w': _L1_xattn_in['a2_li2_w'], 'L1_xattn_a2_li2_b': _L1_xattn_in['a2_li2_b'], 'L1_xattn_a2_li3_w': _L1_xattn_in['a2_li3_w'], 'L1_xattn_a2_li3_b': _L1_xattn_in['a2_li3_b'], 'L1_ffn_Wg': _L1_ffn_in['Wg'], 'L1_ffn_w1': _L1_ffn_in['w1'], 'L1_ffn_w2': _L1_ffn_in['w2']}

def reference(x, ctx_512, L0_xattn_Wq, L0_xattn_Wkv, L0_xattn_Wo, L0_ffn_router_w, L0_ffn_w1, L0_ffn_b1, L0_ffn_w2, L0_ffn_b2, L1_xattn_ln1_g, L1_xattn_ln1_b, L1_xattn_ln2_g, L1_xattn_ln2_b, L1_xattn_a1_wq, L1_xattn_a1_wk, L1_xattn_a1_wv, L1_xattn_a1_li1_w, L1_xattn_a1_li1_b, L1_xattn_a1_lnx_g, L1_xattn_a1_lnx_b, L1_xattn_a1_lny_g, L1_xattn_a1_lny_b, L1_xattn_a1_ln3_g, L1_xattn_a1_ln3_b, L1_xattn_a1_li2_w, L1_xattn_a1_li2_b, L1_xattn_a1_li3_w, L1_xattn_a1_li3_b, L1_xattn_a2_wq, L1_xattn_a2_wk, L1_xattn_a2_wv, L1_xattn_a2_li1_w, L1_xattn_a2_li1_b, L1_xattn_a2_lnx_g, L1_xattn_a2_lnx_b, L1_xattn_a2_lny_g, L1_xattn_a2_lny_b, L1_xattn_a2_ln3_g, L1_xattn_a2_ln3_b, L1_xattn_a2_li2_w, L1_xattn_a2_li2_b, L1_xattn_a2_li3_w, L1_xattn_a2_li3_b, L1_ffn_Wg, L1_ffn_w1, L1_ffn_w2):
    import jax
    import jax.numpy as jnp

    def _L0_xattn_ref(x, z, Wq, Wkv, Wo):
        import jax, jax.numpy as jnp
        import numpy as np
        DIM = 256
        LATENT_DIM = 128
        NUM_HEADS = 16
        HEAD_DIM = DIM // NUM_HEADS
        SCALE = HEAD_DIM ** (-0.5)
        B, xN, _ = x.shape
        _, zN, _ = z.shape
        Q = (x @ Wq.T).reshape(B, xN, NUM_HEADS, HEAD_DIM)
        KV = (z @ Wkv.T).reshape(B, zN, 2, NUM_HEADS, HEAD_DIM)
        K = KV[:, :, 0]
        V = KV[:, :, 1]
        attn = jnp.einsum('bqhd,bkhd->bhqk', Q, K) * SCALE
        attn = jax.nn.softmax(attn, axis=-1)
        O = jnp.einsum('bhqk,bkhd->bqhd', attn, V).reshape(B, xN, DIM)
        return O @ Wo.T

    def _L0_ffn_ref(hidden_states, router_w, w1, b1, w2, b2):
        import jax, jax.numpy as jnp
        import numpy as np
        S, B, H, F, E, K = (512, 2, 256, 512, 8, 2)

        def _moe_forward(hidden_states, router_w, w1, b1, w2, b2):
            s, b, h = hidden_states.shape
            T = s * b
            x = hidden_states.reshape(T, h)
            logits = jnp.einsum('th,eh->te', x, router_w)
            topk_logits, topk_idx = jax.lax.top_k(logits, K)
            probs = jax.nn.softmax(topk_logits, axis=-1)
            combine = jnp.zeros((T, E), dtype=x.dtype)
            combine = combine.at[jnp.arange(T)[:, None], topk_idx].add(probs.astype(x.dtype))
            hmid = jnp.einsum('th,efh->etf', x, w1) + b1[:, None, :]
            hmid = jax.nn.gelu(hmid, approximate=False)
            y = jnp.einsum('etf,ehf->eth', hmid, w2) + b2[:, None, :]
            out = jnp.einsum('eth,te->th', y, combine)
            return out.reshape(s, b, h)
        return _moe_forward(hidden_states, router_w, w1, b1, w2, b2)

    def _L1_xattn_ref(xx, ee, ln1_g, ln1_b, ln2_g, ln2_b, a1_wq, a1_wk, a1_wv, a1_li1_w, a1_li1_b, a1_lnx_g, a1_lnx_b, a1_lny_g, a1_lny_b, a1_ln3_g, a1_ln3_b, a1_li2_w, a1_li2_b, a1_li3_w, a1_li3_b, a2_wq, a2_wk, a2_wv, a2_li1_w, a2_li1_b, a2_lnx_g, a2_lnx_b, a2_lny_g, a2_lny_b, a2_ln3_g, a2_ln3_b, a2_li2_w, a2_li2_b, a2_li3_w, a2_li3_b, training):
        import jax, jax.numpy as jnp
        import numpy as np
        H, D, C1, C2, S, M, B, W = (16, 32, 256, 128, 512, 128, 2, 4)

        def _ln(x, g, b):
            m = jnp.mean(x, -1, keepdims=True)
            v = jnp.var(x, -1, keepdims=True)
            return (x - m) * jax.lax.rsqrt(v + 1e-05) * g + b

        def _mha(x, y, wq, wk, wv, li1_w, li1_b, lnx_g, lnx_b, lny_g, lny_b, ln3_g, ln3_b, li2_w, li2_b, li3_w, li3_b, causal):
            xn = _ln(x, lnx_g, lnx_b)
            yn = _ln(y, lny_g, lny_b)
            q = jnp.einsum('bsc,hcd->bhsd', xn, wq)
            k = jnp.einsum('btc,hcd->bhtd', yn, wk)
            v = jnp.einsum('btc,hcd->bhtd', yn, wv)
            a = jax.nn.softmax(jnp.einsum('bhsd,bhtd->bhst', q, k) * D ** (-0.5), axis=-1)
            if causal:
                s, t = (a.shape[-2], a.shape[-1])
                mask = (jnp.arange(t)[None, :] > jnp.arange(s)[:, None]).astype(a.dtype)
                a = a * mask
            o = jnp.einsum('bhst,bhtd->bhsd', a, v)
            o = o.transpose(0, 2, 1, 3).reshape(x.shape[0], x.shape[1], H * D)
            x_out = x + o @ li1_w + li1_b
            h = jax.nn.gelu(_ln(x_out, ln3_g, ln3_b) @ li2_w + li2_b, approximate=False)
            return x_out + h @ li3_w + li3_b
        x = _ln(xx, ln1_g, ln1_b)
        x = x + _mha(x, x, a1_wq, a1_wk, a1_wv, a1_li1_w, a1_li1_b, a1_lnx_g, a1_lnx_b, a1_lny_g, a1_lny_b, a1_ln3_g, a1_ln3_b, a1_li2_w, a1_li2_b, a1_li3_w, a1_li3_b, causal=True)
        x = _ln(x, ln2_g, ln2_b)
        return x + _mha(x, ee, a2_wq, a2_wk, a2_wv, a2_li1_w, a2_li1_b, a2_lnx_g, a2_lnx_b, a2_lny_g, a2_lny_b, a2_ln3_g, a2_ln3_b, a2_li2_w, a2_li2_b, a2_li3_w, a2_li3_b, causal=False)

    def _L1_ffn_ref(x, Wg, w1, w2):
        import jax, jax.numpy as jnp
        import numpy as np
        B, T, D = (1, 512, 256)
        E, DFF = (8, 1024)

        def _gating(logits):
            S, num_e = logits.shape
            gates = jax.nn.softmax(logits.astype(jnp.float32), axis=1)
            idx1 = jnp.argmax(gates, axis=1)
            mask1 = jax.nn.one_hot(idx1, num_e, dtype=jnp.int32)
            logits_ex1 = jnp.where(mask1.astype(bool), -jnp.inf, logits)
            idx2 = jnp.argmax(logits_ex1, axis=1)
            mask2 = jax.nn.one_hot(idx2, num_e, dtype=jnp.int32)
            loc1 = jnp.cumsum(mask1, axis=0) - 1
            loc2 = jnp.cumsum(mask2, axis=0) - 1 + jnp.sum(mask1, axis=0, keepdims=True)
            loc1_s = jnp.sum(loc1 * mask1, axis=1)
            loc2_s = jnp.sum(loc2 * mask2, axis=1)
            g1 = jnp.sum(gates * mask1, axis=1)
            g2 = jnp.sum(gates * mask2, axis=1)
            denom = jnp.maximum(g1 + g2, jnp.finfo(jnp.float32).eps)
            g1, g2 = (g1 / denom, g2 / denom)
            cap = S
            loc1_sc = jax.nn.one_hot(loc1_s, cap, dtype=jnp.float32)
            loc2_sc = jax.nn.one_hot(loc2_s, cap, dtype=jnp.float32)
            combine = (g1[:, None] * mask1)[:, :, None] * loc1_sc[:, None, :] + (g2[:, None] * mask2)[:, :, None] * loc2_sc[:, None, :]
            dispatch_mask = combine != 0
            return (combine.astype(logits.dtype), dispatch_mask)
        d_model = x.shape[2]
        xs = x.reshape(-1, d_model)
        logits = xs @ Wg
        combine, dispatch_mask = _gating(logits)
        dispatched = jnp.einsum('sec,sm->ecm', dispatch_mask.astype(jnp.float32), xs)
        expert_out = jax.nn.relu(dispatched @ w1) @ w2
        out = jnp.einsum('sec,ecm->sm', combine, expert_out)
        return out.reshape(x.shape)
    x = x + _L0_xattn_ref(_layernorm(x, axis=-1), ctx_512, L0_xattn_Wq, L0_xattn_Wkv, L0_xattn_Wo)
    x = x + _L0_ffn_ref(_layernorm(x, axis=-1), L0_ffn_router_w, L0_ffn_w1, L0_ffn_b1, L0_ffn_w2, L0_ffn_b2)
    x = x + _L1_xattn_ref(_layernorm(x, axis=-1), ctx_512, L1_xattn_ln1_g, L1_xattn_ln1_b, L1_xattn_ln2_g, L1_xattn_ln2_b, L1_xattn_a1_wq, L1_xattn_a1_wk, L1_xattn_a1_wv, L1_xattn_a1_li1_w, L1_xattn_a1_li1_b, L1_xattn_a1_lnx_g, L1_xattn_a1_lnx_b, L1_xattn_a1_lny_g, L1_xattn_a1_lny_b, L1_xattn_a1_ln3_g, L1_xattn_a1_ln3_b, L1_xattn_a1_li2_w, L1_xattn_a1_li2_b, L1_xattn_a1_li3_w, L1_xattn_a1_li3_b, L1_xattn_a2_wq, L1_xattn_a2_wk, L1_xattn_a2_wv, L1_xattn_a2_li1_w, L1_xattn_a2_li1_b, L1_xattn_a2_lnx_g, L1_xattn_a2_lnx_b, L1_xattn_a2_lny_g, L1_xattn_a2_lny_b, L1_xattn_a2_ln3_g, L1_xattn_a2_ln3_b, L1_xattn_a2_li2_w, L1_xattn_a2_li2_b, L1_xattn_a2_li3_w, L1_xattn_a2_li3_b, 0)
    x = x + _L1_ffn_ref(_layernorm(x, axis=-1), L1_ffn_Wg, L1_ffn_w1, L1_ffn_w2)
    return x

_drawn_inputs = setup_inputs


def setup_inputs(seed=0):
    import zlib

    import numpy as np

    out = dict(_drawn_inputs(seed))
    spreads = {'L0_ffn_b1': (0.0, 0.1),
     'L0_ffn_b2': (0.0, 0.1),
     'L1_xattn_ln1_g': (1.0, 0.2),
     'L1_xattn_ln1_b': (0.0, 0.1),
     'L1_xattn_ln2_g': (1.0, 0.2),
     'L1_xattn_ln2_b': (0.0, 0.1),
     'L1_xattn_a1_li1_b': (0.0, 0.289),
     'L1_xattn_a1_lnx_g': (1.0, 0.6),
     'L1_xattn_a1_lnx_b': (0.0, 0.8),
     'L1_xattn_a1_lny_g': (1.0, 0.6),
     'L1_xattn_a1_lny_b': (0.0, 0.8),
     'L1_xattn_a1_ln3_g': (1.0, 0.6),
     'L1_xattn_a1_ln3_b': (0.0, 2.0),
     'L1_xattn_a1_li2_b': (0.0, 0.75),
     'L1_xattn_a1_li3_b': (0.0, 0.273),
     'L1_xattn_a2_li1_b': (0.0, 0.268),
     'L1_xattn_a2_lnx_g': (1.0, 0.6),
     'L1_xattn_a2_lnx_b': (0.0, 0.8),
     'L1_xattn_a2_lny_g': (1.0, 0.6),
     'L1_xattn_a2_lny_b': (0.0, 0.8),
     'L1_xattn_a2_ln3_g': (1.0, 0.6),
     'L1_xattn_a2_ln3_b': (0.0, 2.0),
     'L1_xattn_a2_li2_b': (0.0, 0.729),
     'L1_xattn_a2_li3_b': (0.0, 0.274)}
    factors = {'L1_xattn_a1_wq': 8.0,
     'L1_xattn_a1_wk': 8.0,
     'L1_xattn_a1_wv': 4.731,
     'L1_xattn_a1_li1_w': 4.734,
     'L1_xattn_a2_wq': 8.0,
     'L1_xattn_a2_wk': 8.0,
     'L1_xattn_a2_wv': 3.277,
     'L1_xattn_a2_li1_w': 3.253,
     'L1_ffn_Wg': 64.0}
    for name, (base, spread) in spreads.items():
        noise = np.random.default_rng([zlib.crc32(name.encode()), seed]).standard_normal(out[name].shape)
        drawn = base * np.exp(spread * noise) if base else spread * noise
        out[name] = jnp.asarray(drawn.astype(out[name].dtype))
    for name, factor in factors.items():
        out[name] = (out[name] * factor).astype(out[name].dtype)
    return out
```

```python
from contextlib import ExitStack

import numpy as np

import concourse.bass as bass
from concourse import mybir
from concourse.alu_op_type import AluOpType as ALU

F32 = mybir.dt.float32
U32 = mybir.dt.uint32
ACT = mybir.ActivationFunctionType
AX = mybir.AxisListType

P = 128
B, S, C = 16, 112, 256
L, D = 375, 128
LK = 125
NK = L // LK
CB = C // P
H = 16
EPS = 1e-5


class Counter:

    def __init__(self, nc, name, per=1, step=1, items=B, follows=None):
        self.sem = follows.sem if follows else nc.alloc_semaphore(name)
        self.base = follows.base + follows.items * follows.per * follows.step if follows else 0
        self.per, self.step, self.items = per, step, items

    def after(self, item, k=None):
        return item * (self.per * self.step) + (self.base + (self.per if k is None else k) * self.step)


def wait(eng, counter, item, k=None):
    value = counter.after(item, k)
    if isinstance(value, int) and value <= counter.base:
        return
    eng.wait_ge(counter.sem, value)


class Pipeline:

    def __init__(self, items):
        self.items, self.actions = items, {}

    def add(self, engine, distance, action):
        self.actions.setdefault(engine, []).append((distance, action))

    def run(self, name, eng):
        todo = self.actions.get(name, [])
        if not todo:
            return
        ahead = max(0, max(d for d, _ in todo))
        behind = max(0, max(-d for d, _ in todo))

        def iteration(it):
            for d, action in todo:
                if not isinstance(it, int) or 0 <= it + d < self.items:
                    action(it + d)

        first, last = behind + 1, self.items - ahead
        if last - first < 2:
            first = last = self.items
        for it in range(-ahead, first):
            iteration(it)
        if last > first:
            with eng.Fori(first, last) as it:
                iteration(it)
        for it in range(last, self.items + behind):
            iteration(it)


class Turns:

    def __init__(self, items, jobs):
        self.items, self.jobs = items, jobs

    def wait_before(self, eng, index, item):
        it = item - self.jobs[index][0]
        for back in range(1, 2 * len(self.jobs) + 1):
            wrap, at = divmod(index - back, len(self.jobs))
            distance, counter, k = self.jobs[at]
            other = it + distance if wrap == 0 else it + (wrap + distance)
            if not isinstance(it, int) or 0 <= other < self.items:
                wait(eng, counter, other, k)
                return



def constants():
    p = np.arange(P)
    parts = dict(
        ident=np.eye(P), ones=np.ones((P, P)),
        mask0=(p[:, None] // 16 == np.arange(8)[None, :]) * (16.0 ** -0.5),
        mask1=(p[:, None] // 32 == np.arange(4)[None, :]) * (32.0 ** -0.5),
        before=(p[:, None] < p[None, :]) * 1.0,
        after=(p[:, None] > p[None, :S]) * 1.0,
        powm=np.full((P, 1), -0.5), eps=np.full((P, 1), EPS),
        iota=np.tile(np.arange(40.0), (P, 1)),
        steps=np.tile(float(P) * np.arange(B * S // P), (P, 1)),
        fresh=np.tile((np.arange(B * E) % B != 0) * 1.0, (P, 1)))
    at, where = 0, {}
    for n, a in parts.items():
        where[n] = (at, at + a.shape[1])
        at += a.shape[1]
    return where, np.concatenate(list(parts.values()), 1).astype(np.float32)


E, F0, TOP = 8, 512, 2
TILES = B * S * TOP // P + E - 1
UNROLL = 5
assert TILES % UNROLL == 0
F1 = 1024
FB = F1 // P
GB = 4
GS = GB * S
CONST_AT, CONST = constants()

COLS = [("a1_lnx_g", 2), ("a1_lnx_b", 2), ("a1_lny_g", 2), ("a1_lny_b", 2), ("a1_ln3_g", 2), ("a1_ln3_b", 2),
        ("a1_li2_b", 8), ("a2_lnx_g", 2), ("a2_lnx_b", 2), ("a2_lny_g", 1), ("a2_lny_b", 1), ("a2_ln3_g", 2),
        ("a2_ln3_b", 2), ("a2_li2_b", 8)]
ROWS = ["ln1_g", "ln1_b", "ln2_g", "ln2_b", "a1_li1_b", "a1_li3_b", "a2_li1_b", "a2_li3_b"]


def carve(region, *shapes):
    at, out = 0, []
    for parts, *free in shapes:
        n = int(np.prod(free))
        assert at + n <= region.shape[1], (at, n)
        v = region[0:parts, at:at + n]
        if len(free) == 2:
            v = v.rearrange("p (a b) -> p a b", a=free[0])
        elif len(free) == 3:
            v = v.rearrange("p (a b c) -> p a b c", a=free[0], b=free[1])
        out.append(v)
        at += n
    return out


def program(nc, t, out, stop=4):
    te, ve, ae, ge, se = nc.tensor, nc.vector, nc.scalar, nc.gpsimd, nc.sync
    with ExitStack() as ctx:
        def sb(name, shape, dt=F32):
            return ctx.enter_context(nc.sbuf_tensor(name, shape, dt))

        X = sb("X", [S, B, C])
        const = sb("const", [P, CONST.shape[1]])
        k = {n: const[:, a:b] for n, (a, b) in CONST_AT.items()}
        ident = k["ident"]
        cols = sb("cols", [P, sum(n for _, n in COLS)])
        at = 0
        for n, w in COLS:
            k[n] = cols[:, at:at + w]
            at += w
        junk, junk2 = sb("junk", [1, 64]), sb("junk2", [1, 64])
        turn = dict(vector=0, gpsimd=0)

        def word(name):
            turn[name] = (turn[name] + 1) % 64
            return slice(turn[name], turn[name] + 1)
        sums = sb("sums", [S, B * H])
        rsum = sb("rsum", [S, H])
        nmax = sb("nmax", [S, H])
        LG = sb("LG", [S, B, E])
        p12 = sb("p12", [S, 2, B])

        first = sb("first", [P, 2048])
        work = sb("work", [P, 10260])
        arena = sb("arena", [P, 26624])
        wa1 = sb("wa1", [P, 8192])
        wq0, wk0, wv0, wo0 = carve(first, (P, CB, C), (P, 1, C), (P, 1, C), (P, CB, C))
        rows = dict(zip(ROWS, carve(first, *[(S, C)] * len(ROWS))))
        w1e, w2e, b1e, b2e, XS = carve(arena, (P, E, CB, F0), (P, E, F0 // P, C), (P, E, F0), (P, E, C), (S, B, C))
        psum = ctx.enter_context(nc.psum_tensor("psum", [P, 8, 512], F32))
        psS, psT, psM, psO = psum[:, 0:4, :], psum[:, 4:6, :], psum[:, 6, :], psum[:, 7, :]

        s_const, s_x, s_w0 = Counter(nc, "const", 2, 16), Counter(nc, "x", 1, 16), Counter(nc, "w0", 5, 16)
        s_out = Counter(nc, "out", B, 16)

        s_x1 = Counter(nc, "x1", 1, 16)
        c_zero, c_fill = Counter(nc, "zero"), Counter(nc, "fill", 1, 16)
        s_we = Counter(nc, "we", 2 + 2 * B, 16)

        def gate(waits):
            for counter, item, k_ in waits:
                wait(ve, counter, item, k_)
            ve.memset(junk[:, word("vector")], 0.0)

        def pool_gate(*waits):
            for counter, item, k_ in waits:
                wait(ge, counter, item, k_)
            ge.tensor_tensor(junk2[:, word("gpsimd")], k["eps"][0:1, :], k["eps"][0:1, :], ALU.add)

        class Norm:

            def __init__(self, tag, rows_=S, blocks=1, follows=None):
                self.rows, self.blocks = rows_, blocks
                self.buf = sb(tag + "_stat", [rows_, blocks * 10])
                b = self.buf
                self.sixes = b[:, 0:6 * blocks].rearrange("p (n s) -> p n s", n=blocks)
                self.mv = b[:, 6 * blocks:8 * blocks].rearrange("p (n s) -> p n s", n=blocks)
                self.veps, self.rstd = b[:, 8 * blocks:9 * blocks], b[:, 9 * blocks:10 * blocks]
                c = lambda name, per=1: Counter(nc, tag + "_" + name, per,
                                                follows=follows and follows.counters[name])
                self.counters = dict(bn=c("bn"), mv=c("mv"), rs=c("rs", 2), xh=c("xh"))
                self.c_bn, self.c_mv, self.c_rs, self.c_xh = self.counters.values()

            def bn_stats(self, b, src, ready):
                gate(ready + [(self.c_mv, b - 1, None)])
                for n in range(self.blocks):
                    ins = ve.bn_stats(self.sixes[:, n, :], src[:, n, :] if self.blocks > 1 else src)
                ins.then_inc(self.c_bn.sem, 1)

            def bn_aggr(self, b):
                gate([(self.c_bn, b, None), (self.c_rs, b - 1, None), (self.c_xh, b - 1, None)])
                for n in range(self.blocks):
                    ins = ve.bn_aggr(self.mv[:, n, :], self.sixes[:, n, :])
                ins.then_inc(self.c_mv.sem, 1)

            def power(self, b):
                r, n = self.rows, self.blocks
                wait(ge, self.c_mv, b)
                ge.tensor_tensor(self.veps, self.mv[:, :, 1], k["eps"][0:r, :].broadcast_to([r, n]),
                                 ALU.add).then_inc(self.c_rs.sem, 1)
                wait(ge, self.c_rs, b, 1)
                wait(ge, self.c_xh, b - 1)
                ge.tensor_tensor(self.rstd, self.veps, k["powm"][0:r, :].broadcast_to([r, n]),
                                 ALU.pow).then_inc(self.c_rs.sem, 1)

            def apply(self, b, src, dst, free):
                wait(ve, self.c_rs, b)
                for counter, item, k_ in free:
                    wait(ve, counter, item, k_)
                for n in range(self.blocks):
                    a, d = (src[:, n, :], dst[:, n, :]) if self.blocks > 1 else (src, dst)
                    ins = ve.tensor_scalar(d, a, self.mv[:, n, 0:1], self.rstd[:, n:n + 1],
                                           ALU.subtract, ALU.mult)
                ins.then_inc(self.c_xh.sem, 1)

            def plan(self, pipe, distance, src, ready):
                pipe.add("vector", distance, lambda b: self.bn_stats(b, src(b), ready(b)))
                pipe.add("vector", distance, lambda b: self.bn_aggr(b))
                pipe.add("gpsimd", distance, lambda b: self.power(b))

            def plan_apply(self, pipe, distance, src, dst, free):
                pipe.add("vector", distance, lambda b: self.apply(b, src(b), dst(b), free(b)))

        def once(b, waits):
            return waits if isinstance(b, int) and b == 0 else []

        def transpose_blocks(src, n, rows_, bank=None):
            bank = psM if bank is None else bank
            for cb in range(n):
                ins = te.transpose(bank[:, cb * rows_:(cb + 1) * rows_], src[:, cb * P:(cb + 1) * P],
                                   ident[0:rows_, 0:rows_])
            return ins

        def psum_rows(n, width, bank=None):
            return (psM if bank is None else bank)[:, 0:n * width].rearrange("p (n w) -> p n w", n=n)

        class Cross:
            def __init__(self, tag, dh, wq, wk, wv, mask, ctx_step=16, follows=None):
                self.tag, self.dh, self.wq, self.wk, self.wv, self.mask = tag, dh, wq, wk, wv, mask
                self.G = P // dh
                self.chunks = H // self.G
                HD = H * dh
                (self.Qb, self.KT, self.V, self.Pr, self.PT, self.xh, self.xT, self.On, self.OT, self.ctxT,
                 self.cx, self.cxh) = carve(
                    work, (P, self.chunks, self.G, S), (P, self.chunks, L), (LK, NK, HD), (S, 4, L), (LK, 4, NK * S),
                    (S, C), (P, CB, S), (S, HD), (P, HD // P, S), (P, L), (LK, NK, D), (LK, NK, D))
                n = self.chunks
                self.counters = {}

                def c(name, per=1, step=1):
                    old = follows.counters[name] if follows and name in follows.counters else None
                    self.counters[name] = Counter(nc, tag + "_" + name, per, step, follows=old)
                    return self.counters[name]
                self.c = c
                self.BY_ACT = [3, 7, 11, 15]
                self.ctx = c("ctx", 1, ctx_step)
                self.xt, self.xtv = c("xt"), c("xtv")
                self.qp, self.q, self.kp, self.kt, self.vp, self.v = (c(x, n) for x in ("qp", "q", "kp", "kt", "vp", "v"))
                self.s, self.mx, self.e = c("s", H), c("mx", H // 2), c("e", H)
                self.tr, self.pv = c("tr", H), c("pv", H)
                self.pta, self.ptv = c("pta", len(self.BY_ACT)), c("ptv", H - len(self.BY_ACT))
                self.rcp, self.on, self.ot, self.otv = c("rcp"), c("on"), c("ot"), c("otv")

            def pt_copied(self, eng, b, h):
                if h < 0:
                    b, h = b - 1, h + H
                if h in self.BY_ACT:
                    wait(eng, self.pta, b, self.BY_ACT.index(h) + 1)
                else:
                    wait(eng, self.ptv, b, h + 1 - sum(x < h for x in self.BY_ACT))

            def scores(self, b, h):
                c, g = divmod(h, self.G)
                if g == 0:
                    wait(te, self.q, b, c + 1)
                    wait(te, self.kt, b, c + 1)
                wait(te, self.e, b, h + 1 - 4)
                te.matmul(psS[0:S, h % 4, 0:L], self.Qb[:, c, g, :], self.KT[:, c, :],
                          start=True, stop=True).then_inc(self.s.sem, 1)

            def row_max(self, b, pair):
                h = 2 * pair
                wait(ve, self.s, b, h + 2)
                ve.tensor_reduce(nmax[:, h:h + 2], psS[0:S, h % 4:h % 4 + 2, 0:L],
                                 AX.X, ALU.max, negate=True).then_inc(self.mx.sem, 1)

            def numerators(self, b, h):
                if h % 2 == 0:
                    wait(ae, self.mx, b, h // 2 + 1)
                wait(ae, self.tr, b, h + 1 - 4)
                ae.activation(self.Pr[:, h % 4, :], psS[0:S, h % 4, 0:L], ACT.Exp, bias=nmax[:, h:h + 1],
                              accum_out=sums[:, bass.ds(b * H + h, 1)]).then_inc(self.e.sem, 1)

            def transpose_numerators(self, b, h):
                wait(te, self.e, b, h + 1)
                self.pt_copied(te, b, h - 2)
                for kb in range(NK):
                    ins = te.transpose(psT[0:LK, h % 2, kb * S:(kb + 1) * S],
                                       self.Pr[:, h % 4, kb * LK:(kb + 1) * LK], ident[0:S, 0:S])
                ins.then_inc(self.tr.sem, 1)

            def copy_transposed(self, b, h):
                eng = ae if h in self.BY_ACT else ve
                wait(eng, self.tr, b, h + 1)
                wait(eng, self.pv, b, h + 1 - 4)
                dst, src = self.PT[:, h % 4, :], psT[0:LK, h % 2, 0:NK * S]
                if eng is ae:
                    ae.activation(dst, src, ACT.Copy).then_inc(self.pta.sem, 1)
                else:
                    ve.tensor_copy(dst, src).then_inc(self.ptv.sem, 1)

            def weigh_values(self, b, h):
                dh = self.dh
                self.pt_copied(te, b, h)
                if h % self.G == 0:
                    wait(te, self.v, b, h // self.G + 1)
                if h == 0:
                    wait(te, self.on, b - 1)
                for kb in range(NK):
                    ins = te.matmul(psO[0:S, h * dh:(h + 1) * dh], self.PT[:, h % 4, kb * S:(kb + 1) * S],
                                    self.V[:, kb, h * dh:(h + 1) * dh], start=kb == 0, stop=kb == NK - 1)
                ins.then_inc(self.pv.sem, 1)

            def queries(self, b, c):
                wait(te, self.xtv, b)
                for cb in range(CB):
                    ins = te.matmul(psM[:, 0:S], self.wq[:, cb, c * P:(c + 1) * P], self.xT[:, cb, :],
                                    start=cb == 0, stop=cb == CB - 1)
                ins.then_inc(self.qp.sem, 1)

            def spread_queries(self, b, c):
                wait(ve, self.qp, b, c + 1)
                wait(ve, self.s, b - 1, self.G * (c + 1))
                ve.tensor_tensor(self.Qb[:, c, :, :], psM[:, 0:S].unsqueeze(1).broadcast_to([P, self.G, S]),
                                 self.mask.unsqueeze(2).broadcast_to([P, self.G, S]), ALU.mult).then_inc(self.q.sem, 1)

            def keys(self, b, c):
                wait(te, self.ctx, b)
                te.matmul(psM[:, 0:L], self.wk[:, 0, c * P:(c + 1) * P], self.ctxT, start=True, stop=True)\
                  .then_inc(self.kp.sem, 1)

            def copy_keys(self, b, c):
                wait(ae, self.kp, b, c + 1)
                wait(ae, self.s, b - 1, self.G * (c + 1))
                ae.activation(self.KT[:, c, :], psM[:, 0:L], ACT.Copy).then_inc(self.kt.sem, 1)

            def values(self, b, c):
                for kb in range(NK):
                    ins = te.matmul(psM[0:LK, kb * P:(kb + 1) * P], self.ctxT[:, kb * LK:(kb + 1) * LK],
                                    self.wv[:, 0, c * P:(c + 1) * P], start=True, stop=True)
                ins.then_inc(self.vp.sem, 1)

            def copy_values(self, b, c):
                wait(ve, self.vp, b, c + 1)
                wait(ve, self.pv, b - 1, self.G * (c + 1))
                ve.tensor_copy(self.V[:, :, c * P:(c + 1) * P],
                               psM[0:LK, 0:NK * P].rearrange("p (n m) -> p n m", n=NK)).then_inc(self.v.sem, 1)

            def transpose_o(self, b):
                wait(te, self.on, b)
                transpose_blocks(self.On, H * self.dh // P, S).then_inc(self.ot.sem, 1)

            def copy_o(self, b):
                wait(ae, self.ot, b)
                n = H * self.dh // P
                ae.activation(self.OT[:, :, :], psM[:, 0:n * S], ACT.Copy).then_inc(self.otv.sem, 1)

            def recip_sums(self, b):
                wait(ve, self.e, b)
                wait(ve, self.on, b - 1)
                ve.reciprocal(rsum[:, :], sums[:, bass.ds(b * H, H)]).then_inc(self.rcp.sem, 1)

            def divide(self, b):
                wait(ve, self.rcp, b)
                wait(ve, self.pv, b)
                wait(ve, self.ot, b - 1)
                n = H * self.dh
                ve.tensor_tensor(self.On.rearrange("p (h d) -> p h d", h=H),
                                 psO[0:S, 0:n].rearrange("p (h d) -> p h d", h=H),
                                 rsum[:, :].unsqueeze(2).broadcast_to([S, H, self.dh]), ALU.mult).then_inc(self.on.sem, 1)

            def plan(self, pipe, jobs, extra, LT=4, LP=6):
                turns = Turns(B, [(d, counter, ev) for _, d, _, _, _, counter, ev in jobs])
                for h in range(H):
                    at = lambda lag: (0 if h >= lag else -1, (h - lag) % H)
                    pipe.add("tensor", 0, lambda b, h=h: self.scores(b, h))
                    d, g = at(LT)
                    pipe.add("tensor", d, lambda b, g=g: self.transpose_numerators(b, g))
                    if h % 2 == 1:
                        pipe.add("vector", 0, lambda b, h=h: self.row_max(b, h // 2))
                        pipe.add("scalar", 0, lambda b, h=h: self.numerators(b, h - 1))
                        pipe.add("scalar", 0, lambda b, h=h: self.numerators(b, h))
                    pipe.add("scalar" if g in self.BY_ACT else "vector", d, lambda b, g=g: self.copy_transposed(b, g))
                    d, g = at(LP)
                    pipe.add("tensor", d, lambda b, g=g: self.weigh_values(b, g))
                    if h == 5:
                        pipe.add("vector", -1, self.recip_sums)
                        pipe.add("vector", -1, self.divide)
                    for n, (step, d, pe, who, copy, counter, ev) in enumerate(jobs):
                        if step == h:
                            def job(b, n=n, pe=pe):
                                turns.wait_before(te, n, b)
                                pe(b)
                            pipe.add("tensor", d, job)
                            pipe.add(who, d, copy)
                    for step, who, d, action in extra:
                        if step == h:
                            pipe.add(who, d, action)

        a0 = Pipeline(B)
        x0 = Cross("a0", 16, wq0, wk0, wv0, k["mask0"])
        wo_p, res0 = x0.c("wo"), x0.c("res")
        n0, nr = Norm("n0"), Norm("nr")
        xr, xTr = carve(wa1[:, 1024:1536], (S, C), (P, CB, S))
        rw = sb("rw", [P, CB, E])
        rt, rtv, rl, rlv = x0.c("rt"), x0.c("rtv"), x0.c("rl"), x0.c("rlv")

        def load_ctxT(b):
            wait(se, x0.vp, b - 1)
            se.dma_start(x0.ctxT, t["ctxT"][b, :, :]).then_inc(x0.ctx.sem, 16)

        def transpose_rows0(b):
            wait(te, n0.c_xh, b)
            transpose_blocks(x0.xh, CB, S).then_inc(x0.xt.sem, 1)

        def copy_rows0(b):
            wait(ae, x0.xt, b)
            ae.activation(x0.xT, psum_rows(CB, S), ACT.Copy).then_inc(x0.xtv.sem, 1)

        def project_o0(b):
            wait(te, x0.otv, b)
            for cb in range(CB):
                ins = te.matmul(psM[0:S, 0:C], x0.OT[:, cb, :], wo0[:, cb, :], start=cb == 0, stop=cb == CB - 1)
            ins.then_inc(wo_p.sem, 1)

        def add_residual0(b):
            wait(ve, wo_p, b)
            ve.tensor_tensor(X[:, b, :], psM[0:S, 0:C], X[:, b, :], ALU.add).then_inc(res0.sem, 1)

        def copy_router(b):
            wait(ae, rt, b)
            wait(ae, rl, b - 1)
            ae.activation(xTr, psum_rows(CB, S), ACT.Copy).then_inc(rtv.sem, 1)

        def logits0(b):
            wait(te, rtv, b)
            for cb in range(CB):
                ins = te.matmul(psM[0:S, 0:E], xTr[:, cb, :], rw[:, cb, :], start=cb == 0, stop=cb == CB - 1)
            ins.then_inc(rl.sem, 1)

        def copy_logits0(b):
            wait(ve, rl, b)
            ve.tensor_copy(LG[:, b, :], psM[0:S, 0:E]).then_inc(rlv.sem, 1)

        c_xs = Counter(nc, "xs")

        def keep_rows(b):
            for counter, item, k_ in once(b, [(c_fill, 3, None)]):
                wait(ge, counter, item, k_)
            wait(ge, nr.c_xh, b)
            ge.tensor_copy(XS[:, b, :], xr).then_inc(c_xs.sem, 1)

        def transpose_router(b):
            wait(te, nr.c_xh, b)
            transpose_blocks(xr, CB, S).then_inc(rt.sem, 1)
        J = lambda f, c: (lambda b: f(b, c))
        jobs0 = [(0, 0, J(x0.queries, 1), "vector", J(x0.spread_queries, 1), x0.q, 2),
                 (1, 0, J(x0.keys, 1), "scalar", J(x0.copy_keys, 1), x0.kt, 2),
                 (4, 1, transpose_rows0, "scalar", copy_rows0, x0.xtv, 1),
                 (6, 0, J(x0.values, 1), "vector", J(x0.copy_values, 1), x0.v, 2),
                 (7, -1, x0.transpose_o, "scalar", x0.copy_o, x0.otv, 1),
                 (8, -1, project_o0, "vector", add_residual0, res0, 1),
                 (9, 1, J(x0.queries, 0), "vector", J(x0.spread_queries, 0), x0.q, 1),
                 (10, 1, J(x0.keys, 0), "scalar", J(x0.copy_keys, 0), x0.kt, 1),
                 (12, -1, transpose_router, "scalar", copy_router, rtv, 1),
                 (14, 1, J(x0.values, 0), "vector", J(x0.copy_values, 0), x0.v, 1),
                 (15, -1, logits0, "vector", copy_logits0, rlv, 1)]
        rowsX = lambda b: X[:, b, :]
        extra0 = [(0, "vector", 1, lambda b: n0.bn_stats(b, rowsX(b), once(b, [(s_x, 0, None)]) + once(b - 1, [(s_x1, 0, None)]))),
                  (0, "vector", 1, lambda b: n0.bn_aggr(b)), (0, "gpsimd", 1, lambda b: n0.power(b)),
                  (2, "vector", 1, lambda b: n0.apply(b, rowsX(b), x0.xh, [(x0.xt, b - 1, None)])),
                  (8, "vector", -1, lambda b: nr.bn_stats(b, rowsX(b), [(res0, b, None)])),
                  (8, "vector", -1, lambda b: nr.bn_aggr(b)), (8, "gpsimd", -1, lambda b: nr.power(b)),
                  (10, "vector", -1, lambda b: nr.apply(b, rowsX(b), xr, [(rt, b - 1, None), (c_xs, b - 1, None)])),
                  (10, "gpsimd", -1, keep_rows)]
        def load_experts(b):
            se.dma_start(w1e.rearrange("p e n m -> p (e n) m")[:, b, :],
                         t["w1e"].rearrange("e (n p) m -> (e n) p m", p=P)[b, :, :]).then_inc(s_we.sem, 16)
            se.dma_start(w2e.rearrange("p e (a n) m -> p (e a) n m", n=2)[:, b, :, :],
                         t["w2e"].rearrange("e (a n p) m -> (e a) p n m", p=P, n=2)[b, :, :, :]).then_inc(s_we.sem, 16)
        a0.add("sync", 1, load_ctxT)
        a0.add("sync", 0, load_experts)
        a0.add("tensor", 1, lambda b: once(b, [0]) and wait(te, s_w0, 0))
        x0.plan(a0, jobs0, extra0)

        class Chain:

            def __init__(self, tag, eng):
                self.c, self.n, self.eng = Counter(nc, tag), 0, eng

            def __call__(self, ins):
                ins.then_inc(self.c.sem, 1)
                self.n += 1
                return self.n

            def settle(self):
                self.eng.wait_ge(self.c.sem, self.n)

        BE = B * E
        (eq, cand, oh1, oh2, lg2, MS, tot, incl, pos, prod, cm, m1, m2, posk, cmp_, nt, ntc, st, cmp2, eidf, dd) = carve(
            work, *[(S, B, E)] * 5, *[(S, E, B)] * 4, (S, B, E), *[(S, B)] * 4, (S, E, B * S // P), (S, E), (S, E), (S, E),
            (1, 40, E - 1), (1, 40), (S, B))
        idx_all = sb("idx", [S, TOP, B], U32)
        idx = [idx_all[:, n, :] for n in range(TOP)]
        idx_b = sb("idx_b", [S, TOP, 1], U32)
        eid = sb("eid", [1, 40], U32)
        slots_x, slots_y = t["slots_x"], t["slots_y"]
        c_ms, c_rank, c_dd, c_ee, c_idx = (Counter(nc, x) for x in ("ms", "rank", "dd", "ee", "idx"))
        chain = Chain("route", ve)
        eb = lambda a: a.rearrange("p e b -> p b e")
        over_e = lambda a: a.unsqueeze(2).broadcast_to([S, B, E])
        over_b = lambda a: a.unsqueeze(2).broadcast_to([S, E, B])

        def top_two(step):
            iota8 = k["iota"][0:S, 0:E].unsqueeze(1).broadcast_to([S, B, E])
            src = LG[:, :, :]
            for m, oh in ((m1, oh1), (m2, oh2)):
                step(ve.tensor_reduce(m, src, AX.X, ALU.max))
                step(ve.tensor_tensor(eq, src, over_e(m), ALU.is_equal))
                step(ve.scalar_tensor_tensor(cand, eq, -100.0, iota8, ALU.mult, ALU.add))
                step(ve.tensor_reduce(cm, cand, AX.X, ALU.min))
                step(ve.tensor_tensor(oh, cand, over_e(cm), ALU.is_equal))
                if oh is oh1:
                    step(ve.scalar_tensor_tensor(lg2, oh1, -3.0e38, LG[:, :, :], ALU.mult, ALU.add))
                    src = lg2

        def route_vector():
            def step(ins):
                chain(ins)
                chain.settle()
            wait(ve, rlv, B - 1)
            top_two(step)
            step(ve.tensor_tensor(eb(MS), oh1, oh2, ALU.add))
            ve.tensor_tensor(dd, m2, m1, ALU.subtract).then_inc(c_dd.sem, 1)
            ve.wait_ge(c_rank.sem, 1)
            flat = lambda a: a.rearrange("p e b -> p (e b)")
            step(ve.tensor_copy(tot, psM[0:S, BE:2 * BE].rearrange("p (e b) -> p e b", e=E)))
            step(ve.tensor_tensor_scan(flat(incl), k["fresh"][0:S, :], flat(tot), 0.0, ALU.mult, ALU.add))
            step(ve.tensor_tensor(pos, incl, tot, ALU.subtract))
            step(ve.tensor_tensor(flat(pos), psM[0:S, 0:BE], flat(pos), ALU.add))
            n = B * S // P
            step(ve.tensor_tensor(cmp_, incl[:, :, B - 1:B].broadcast_to([S, E, n]),
                                  k["steps"][0:S, :].unsqueeze(1).broadcast_to([S, E, n]), ALU.is_gt))
            step(ve.tensor_reduce(nt, cmp_, AX.X, ALU.add))
            step(ve.tensor_tensor_scan(ntc, k["ones"][0:S, 0:E], nt, 0.0, ALU.mult, ALU.add))
            step(ve.tensor_tensor(st, ntc, nt, ALU.subtract))
            step(ve.scalar_tensor_tensor(pos, over_b(st), float(P), pos, ALU.mult, ALU.add))
            for oh, ix in ((oh1, idx[0]), (oh2, idx[1])):
                step(ve.tensor_tensor(prod, oh, eb(pos), ALU.mult))
                step(ve.tensor_reduce(posk, prod, AX.X, ALU.add))
                step(ve.tensor_copy(ix, posk))
            step(ve.tensor_tensor(cmp2, k["iota"][0:1, :].unsqueeze(2).broadcast_to([1, 40, E - 1]),
                                  ntc[0:1, 0:E - 1].unsqueeze(1).broadcast_to([1, 40, E - 1]), ALU.is_ge))
            step(ve.tensor_reduce(eidf, cmp2, AX.X, ALU.add))
            step(ve.tensor_copy(eid[:, :], eidf))
            ve.tensor_copy(junk[:, word("vector")], eidf[:, 0:1]).then_inc(c_idx.sem, 1)
            ve.wait_ge(c_ee.sem, 1)
            step(ve.tensor_scalar(p12[:, 0, :], dd, 1.0, None, ALU.add))
            step(ve.reciprocal(p12[:, 0, :], p12[:, 0, :]))
            step(ve.tensor_tensor(p12[:, 1, :], p12[:, 0, :], dd, ALU.mult))

        def route_tensor():
            te.wait_ge(chain.c.sem, 12)
            flat = MS.rearrange("p e b -> p (e b)")
            te.matmul(psM[0:S, 0:BE], k["before"][0:S, 0:S], flat, start=True, stop=True)
            te.matmul(psM[0:S, BE:2 * BE], k["ones"][0:S, 0:S], flat, start=True, stop=True).then_inc(c_rank.sem, 1)

        def route_scalar():
            ae.wait_ge(c_dd.sem, 1)
            ae.activation(dd, dd, ACT.Exp).then_inc(c_ee.sem, 1)

        c_sc = Counter(nc, "scatter", 1, 16)

        def scatter():
            wait(ge, c_fill, 3)
            ge.wait_ge(c_idx.sem, 1)
            wait(ge, c_xs, B - 1)
            for b in range(B):
                for n in range(TOP):
                    ge.indirect_dma_start(slots_x, bass.IndirectOffsetOnAxis(ap=idx[n][:, b:b + 1], axis=0),
                                          XS[:, b, :], None).then_inc(c_sc.sem, 16)

        R = UNROLL
        xg, xgT, hb, hT_, yg = carve(work, (P, R, C), (P, R, CB, P), (P, R, F0), (P, R, F0 // P, P), (P, R, C))
        tiles = Pipeline(TILES // R)
        m_ld, m_st = ([Counter(nc, f"m_{x}{r}", 1, 16) for r in range(R)] for x in ("ld", "st"))
        (m_gt, m_gtv, m_h, m_hb, m_gl, m_ht, m_htv, m_y, m_yg) = (
            Counter(nc, "m_" + x) for x in ("gt", "gtv", "h", "hb", "gl", "ht", "htv", "y", "yg"))
        psGT, psH, psHT, psY = psM, psum, psum[:, 5, :], psO

        def expert(eng, j):
            return eng.value_load(eid[0:1, bass.ds(j, 1)], min_val=0, max_val=E - 1)

        def m_load(j, r, it):
            if isinstance(j, int) and j == 0:
                wait(se, c_sc, TOP * B - 1)
            wait(se, m_gt, j - R)
            se.dma_start(xg[:, r, :], slots_x[bass.ds(j * P, P), :]).then_inc(m_ld[r].sem, 16)

        def m_transpose(j, r, it):
            wait(te, m_ld[r], it)
            wait(te, m_gtv, j - 1)
            for cb in range(CB):
                ins = te.transpose(psGT[:, cb * P:(cb + 1) * P], xg[:, r, cb * P:(cb + 1) * P], ident)
            ins.then_inc(m_gt.sem, 1)

        def m_copy_x(j, r, it):
            wait(ae, m_gt, j)
            wait(ae, m_h, j - R)
            ae.activation(xgT[:, r, :, :], psGT[:, 0:C].rearrange("p (n w) -> p n w", n=CB), ACT.Copy).then_inc(m_gtv.sem, 1)

        def m_up(j, r, it):
            e = expert(te, j)
            if isinstance(j, int) and j == 0:
                wait(te, s_we, 0)
            wait(te, m_gtv, j)
            wait(te, m_hb, j - R)
            for cb in range(CB):
                ins = te.matmul(psH[:, r, :], xgT[:, r, cb, :], w1e[:, e, cb, :], start=cb == 0, stop=cb == CB - 1)
            ins.then_inc(m_h.sem, 1)

        def m_bias_up(j, r, it):
            e = expert(ve, j)
            wait(ve, m_h, j)
            wait(ve, m_ht, j - R)
            ve.tensor_tensor(hb[:, r, :], psH[:, r, :], b1e[:, e, :], ALU.add).then_inc(m_hb.sem, 1)

        def m_gelu(j, r, it):
            wait(ae, m_hb, j)
            ae.activation(hb[:, r, :], hb[:, r, :], ACT.Gelu).then_inc(m_gl.sem, 1)

        def m_transpose_h(j, r, it):
            wait(te, m_gl, j)
            wait(te, m_htv, j - 1)
            for fb in range(F0 // P):
                ins = te.transpose(psHT[:, fb * P:(fb + 1) * P], hb[:, r, fb * P:(fb + 1) * P], ident)
            ins.then_inc(m_ht.sem, 1)

        def m_copy_h(j, r, it):
            wait(ve, m_ht, j)
            wait(ve, m_y, j - R)
            ve.tensor_copy(hT_[:, r, :, :], psHT.rearrange("p (n w) -> p n w", n=F0 // P)).then_inc(m_htv.sem, 1)

        def m_down(j, r, it):
            e = expert(te, j)
            wait(te, m_htv, j)
            wait(te, m_yg, j - 1)
            n = F0 // P
            for fb in range(n):
                ins = te.matmul(psY[:, 0:C], hT_[:, r, fb, :], w2e[:, e, fb, :], start=fb == 0, stop=fb == n - 1)
            ins.then_inc(m_y.sem, 1)

        def m_bias_down(j, r, it):
            e = expert(ve, j)
            wait(ve, m_y, j)
            wait(ve, m_st[r], it - 1)
            ve.tensor_tensor(yg[:, r, :], psY[:, 0:C], b2e[:, e, :], ALU.add).then_inc(m_yg.sem, 1)

        def m_store(j, r, it):
            wait(se, m_yg, j)
            se.dma_start(slots_y[bass.ds(j * P, P), :], yg[:, r, :]).then_inc(m_st[r].sem, 16)

        def tiles_ready(eng):
            eng.wait_ge(c_idx.sem, 1)
        for u in range(R):
            def put(who, f, lag):
                d, r = divmod(u - lag, R)
                tiles.add(who, d, lambda it, f=f, r=r: f(it * R + r, r, it))
            put("sync", m_load, -3)
            put("tensor", m_transpose, -1)
            put("scalar", m_copy_x, -1)
            put("tensor", m_up, 0)
            put("vector", m_bias_up, 0)
            put("scalar", m_gelu, 0)
            put("tensor", m_transpose_h, 1)
            put("vector", m_copy_h, 1)
            put("tensor", m_down, 2)
            put("vector", m_bias_down, 2)
            put("sync", m_store, 2)

        c_g, c_cmb, c_ib = Counter(nc, "gather", TOP, 16), Counter(nc, "combine", TOP), Counter(nc, "idx_b")
        (yk,) = carve(work[:, 8960:9472], (S, TOP, C))

        def gather(b):
            if isinstance(b, int) and b == 0:
                for r in range(R):
                    wait(ge, m_st[r], TILES // R - 1)
            pool_gate((c_cmb, b - 1, None))
            ge.tensor_copy(idx_b[:, :, :], idx_all[:, :, bass.ds(b, 1)]).then_inc(c_ib.sem, 1)
            pool_gate((c_ib, b, None))
            for n in range(TOP):
                ge.indirect_dma_start(yk[:, n, :], None, slots_y,
                                      bass.IndirectOffsetOnAxis(ap=idx_b[:, n, :], axis=0)).then_inc(c_g.sem, 16)

        def combine(b):
            for n in range(TOP):
                if n:
                    wait(ve, c_cmb, b, n)
                else:
                    wait(ve, c_g, b)
                ve.scalar_tensor_tensor(X[:, b, :], yk[:, n, :], p12[:, n, bass.ds(b, 1)], X[:, b, :],
                                        ALU.mult, ALU.add).then_inc(c_cmb.sem, 1)

        (yk_zero,) = carve(arena[:, 22528:26624], (P, 2240))

        def x0_first(eng, dma, blocks):
            dma(X[:, 1:B, :], t["x"][1:B, :, :].rearrange("b s c -> s b c"), s_x1)
            dma(rw[:, :, :], blocks(t["rw"]), s_w0)
            dma(b1e, t["b1e"].partition_broadcast(P), s_we)
            dma(b2e, t["b2e"].partition_broadcast(P), s_we)
            wait(eng, c_zero, 0)
            for n in range(4):
                dma(slots_x.rearrange("(p r) c -> p (r c)", p=P)[:, n * 2240:(n + 1) * 2240], yk_zero, c_fill)
        XA, XO, hT, hid, wq2, wk2, wv2, a2_li1, a2_li2, a2_li3, f1w, f2w = carve(
            arena, (S, B, C), (S, B, C), (P, CB, B * S), (P, FB, GS), (P, CB, 512), (P, 1, 512), (P, 1, 512),
            (P, 4, C), (P, CB, F1), (P, FB, C), (P, CB, F1), (P, FB, C))
        wq1, wk1, wv1, a1_li1, a1_li2, a1_li3 = carve(
            wa1, (P, CB, 512), (P, CB, 512), (P, CB, 512), (P, 4, C), (P, CB, F1), (P, FB, C))
        wg = sb("wg", [P, CB, E])
        s_wa1, s_rows, s_wa2 = Counter(nc, "wa1", 6, 16), Counter(nc, "rows", len(ROWS), 16), Counter(nc, "wa2", 9, 16)
        HB = 512 // P
        XH = lambda cb: slice(cb * P, (cb + 1) * P)

        class Residual:

            def __init__(self, tag, norm, xb, scaled, ln, pre):
                self.norm, self.xb, self.ln, self.pre = norm, xb, ln, pre
                self.xs = scaled
                self.xa, self.fin = Counter(nc, tag + "_xa", 3), Counter(nc, tag + "_fin", 3 if pre == "a2" else 2)

            def affine(self, b, free):
                for counter, item, k_ in once(b, [(s_rows, 0, None)]):
                    wait(ge, counter, item, k_)
                wait(ge, self.norm.c_xh, b)
                ge.tensor_tensor(self.xs, self.xb, rows[self.ln + "_g"], ALU.mult).then_inc(self.xa.sem, 1)
                pool_gate((self.xa, b, 1))
                ge.tensor_tensor(XA[:, b, :], self.xs, rows[self.ln + "_b"], ALU.add).then_inc(self.xa.sem, 1)
                pool_gate((self.xa, b, 2))
                ge.tensor_tensor(XO[:, b, :], XA[:, b, :], rows[self.pre + "_li1_b"], ALU.add).then_inc(self.xa.sem, 1)

            def finish(self, b, norm3):
                pool_gate((norm3.c_xh, b, None))
                ge.tensor_tensor(XO[:, b, :], XO[:, b, :], XA[:, b, :], ALU.add).then_inc(self.fin.sem, 1)
                pool_gate((self.fin, b, 1))
                ge.tensor_tensor(XO[:, b, :], XO[:, b, :], rows[self.pre + "_li3_b"], ALU.add).then_inc(self.fin.sem, 1)
                if self.pre == "a2":
                    pool_gate((self.fin, b, 2))
                    ge.tensor_tensor(XO[:, b, :], XO[:, b, :], X[:, b, :], ALU.add).then_inc(self.fin.sem, 1)

        def affine_copy(dst, src, g, b_, cb):
            return ae.activation(dst, src, ACT.Identity, bias=b_[:, cb:cb + 1], scale=g[:, cb:cb + 1])

        a1 = Pipeline(B)
        Qb, KT1, V1, Pr1, PT1, xh1, xTq, xTy, On1, OT1, y0, xb1, xh3, xs1 = carve(
            work[:, 0:8960], (P, 4, 4, S), (P, 4, S), (S, 512), (S, 2, 4 * S), (S, 2, 4 * S), (S, C), (P, CB, S),
            (P, CB, S), (S, 512), (P, 4, S), (S, C), (S, C), (S, C), (S, C))
        nA, nB, nC, nD = Norm("nA", follows=n0), Norm("nB", follows=nr), Norm("nC"), Norm("nD")
        r1 = Residual("r1", nB, xb1, xs1, "ln1", "a1")
        c = lambda name, per=1, step=1: Counter(nc, "a1_" + name, per, step)
        u_xt, u_xtv, u_qk, u_q, u_k, u_vp, u_v = c("xt"), c("xtv"), c("qk", 4), c("q", 4), c("k", 4), c("vp"), c("v")
        u_s, u_mx, u_e, u_tr, u_pt, u_pv = (c(x, 4) for x in ("s", "mx", "e", "tr", "pt", "pv"))
        u_rcp, u_on, u_ot, u_otv, u_li, u_xo, u_ht, u_htv = (c(x) for x in ("rcp", "on", "ot", "otv", "li", "xo", "ht", "htv"))

        def u_scores(b, g):
            wait(te, u_q, b, g + 1)
            wait(te, u_k, b, g + 1)
            wait(te, u_e, b, g + 1 - 2)
            for i in range(4):
                ins = te.matmul(psS[0:S, g % 2, i * S:(i + 1) * S], Qb[:, g, i, :], KT1[:, g, :], start=True, stop=True)
            ins.then_inc(u_s.sem, 1)

        def u_max(b, g):
            wait(ve, u_s, b, g + 1)
            ve.tensor_reduce(nmax[:, 4 * g:4 * g + 4], psS[0:S, g % 2, 0:4 * S].rearrange("p (h s) -> p h s", h=4),
                             AX.X, ALU.max, negate=True).then_inc(u_mx.sem, 1)

        def u_exp(b, g):
            wait(ae, u_mx, b, g + 1)
            wait(ae, u_tr, b, g + 1 - 2)
            for i in range(4):
                h = 4 * g + i
                ins = ae.activation(Pr1[:, g % 2, i * S:(i + 1) * S], psS[0:S, g % 2, i * S:(i + 1) * S], ACT.Exp,
                                    bias=nmax[:, h:h + 1], accum_out=sums[:, bass.ds(b * H + h, 1)])
            ins.then_inc(u_e.sem, 1)

        def u_transpose(b, g):
            wait(te, u_e, b, g + 1)
            wait(te, u_pt, b, g + 1 - 2)
            for i in range(4):
                ins = te.transpose(psT[0:S, g % 2, i * S:(i + 1) * S], Pr1[:, g % 2, i * S:(i + 1) * S], ident[0:S, 0:S])
            ins.then_inc(u_tr.sem, 1)

        def u_mask(b, g):
            wait(ve, u_tr, b, g + 1)
            wait(ve, u_pv, b, g + 1 - 2)
            ve.tensor_tensor(PT1[:, g % 2, :].rearrange("p (h s) -> p h s", h=4),
                             psT[0:S, g % 2, 0:4 * S].rearrange("p (h s) -> p h s", h=4),
                             k["after"][0:S, :].unsqueeze(1).broadcast_to([S, 4, S]), ALU.mult).then_inc(u_pt.sem, 1)

        def u_values(b, g):
            wait(te, u_pt, b, g + 1)
            if g == 0:
                wait(te, u_v, b)
                wait(te, u_on, b - 1)
            for i in range(4):
                h = 4 * g + i
                ins = te.matmul(psO[0:S, h * 32:(h + 1) * 32], PT1[:, g % 2, i * S:(i + 1) * S],
                                V1[:, h * 32:(h + 1) * 32], start=True, stop=True)
            ins.then_inc(u_pv.sem, 1)

        def u_recip(b):
            wait(ve, u_e, b)
            wait(ve, u_on, b - 1)
            ve.reciprocal(rsum[:, :], sums[:, bass.ds(b * H, H)]).then_inc(u_rcp.sem, 1)

        def u_divide(b):
            wait(ve, u_rcp, b)
            wait(ve, u_pv, b)
            wait(ve, u_ot, b - 1)
            ve.tensor_tensor(On1.rearrange("p (h d) -> p h d", h=H), psO[0:S, :].rearrange("p (h d) -> p h d", h=H),
                             rsum[:, :].unsqueeze(2).broadcast_to([S, H, 32]), ALU.mult).then_inc(u_on.sem, 1)

        def u_vproj(b, bank):
            for cb in range(CB):
                ins = te.matmul(bank[0:S, :], xTy[:, cb, :], wv1[:, cb, :], start=cb == 0, stop=cb == CB - 1)
            ins.then_inc(u_vp.sem, 1)

        def u_vcopy(b, bank):
            wait(ae, u_vp, b)
            wait(ae, u_pv, b - 1)
            ae.activation(V1, bank[0:S, :], ACT.Copy).then_inc(u_v.sem, 1)

        def u_xtr(b, bank):
            wait(te, nC.c_xh, b)
            transpose_blocks(xh1, CB, S, bank).then_inc(u_xt.sem, 1)

        def u_xcopy(b, bank):
            wait(ae, u_xt, b)
            for cb in range(CB):
                affine_copy(xTq[:, cb, :], bank[:, cb * S:(cb + 1) * S], k["a1_lnx_g"], k["a1_lnx_b"], cb)
                ins = affine_copy(xTy[:, cb, :], bank[:, cb * S:(cb + 1) * S], k["a1_lny_g"], k["a1_lny_b"], cb)
            ins.then_inc(u_xtv.sem, 1)

        def u_qkproj(b, bank, g):
            wait(te, u_xtv, b)
            for at_, w, x in ((0, wq1, xTq), (S, wk1, xTy)):
                for cb in range(CB):
                    ins = te.matmul(bank[:, at_:at_ + S], w[:, cb, XH(g)], x[:, cb, :], start=cb == 0, stop=cb == CB - 1)
            ins.then_inc(u_qk.sem, 1)

        def u_qcopy(b, bank, g):
            wait(ve, u_qk, b, g + 1)
            wait(ve, u_k, b, g + 1)
            wait(ve, u_s, b - 1, g + 1)
            ve.tensor_tensor(Qb[:, g, :, :], bank[:, 0:S].unsqueeze(1).broadcast_to([P, 4, S]),
                             k["mask1"].unsqueeze(2).broadcast_to([P, 4, S]), ALU.mult).then_inc(u_q.sem, 1)

        def u_kcopy(b, bank, g):
            wait(ae, u_qk, b, g + 1)
            wait(ae, u_s, b - 1, g + 1)
            ae.activation(KT1[:, g, :], bank[:, S:2 * S], ACT.Copy).then_inc(u_k.sem, 1)

        def u_otr(b, bank):
            wait(te, u_on, b)
            transpose_blocks(On1, HB, S, bank).then_inc(u_ot.sem, 1)

        def u_ocopy(b, bank):
            wait(ae, u_ot, b)
            ae.activation(OT1, psum_rows(HB, S, bank), ACT.Copy).then_inc(u_otv.sem, 1)

        def project_out(OT_, w, copied, counter):
            def action(b, bank=psM):
                wait(te, copied, b)
                for cb in range(HB):
                    ins = te.matmul(bank[0:S, 0:C], OT_[:, cb, :], w[:, cb, :], start=cb == 0, stop=cb == HB - 1)
                ins.then_inc(counter.sem, 1)
            return action

        def add_out(li, res, counter):
            def action(b, bank=psM):
                wait(ve, li, b)
                wait(ve, res.xa, b)
                ve.tensor_tensor(XO[:, b, :], bank[0:S, 0:C], XO[:, b, :], ALU.add).then_inc(counter.sem, 1)
            return action

        def transpose_h(norm, xh_, counter):
            def action(b, bank=psM):
                wait(te, norm.c_xh, b)
                transpose_blocks(xh_, CB, S, bank).then_inc(counter.sem, 1)
            return action

        def copy_h(done, tag, counter):
            def action(b, bank=psM):
                wait(ae, done, b)
                for cb in range(CB):
                    ins = affine_copy(hT[:, cb, bass.ds(b * S, S)], bank[:, cb * S:(cb + 1) * S],
                                      k[tag + "_ln3_g"], k[tag + "_ln3_b"], cb)
                ins.then_inc(counter.sem, 1)
            return action

        G = lambda f, g: (lambda b: f(b, g))
        GJ = lambda f, g: (lambda b, bank: f(b, bank, g))
        QK = lambda g, at_, d: (at_, d, GJ(u_qkproj, g), [("scalar", GJ(u_kcopy, g)), ("vector", GJ(u_qcopy, g))], u_q, g + 1)
        jobs1 = [QK(2, "0B", 0),
                 QK(3, "0C", 0),
                 ("1A", -2, transpose_h(nD, xh3, u_ht), [("scalar", copy_h(u_ht, "a1", u_htv))], u_htv, 1),
                 ("1C", 0, u_vproj, [("scalar", u_vcopy)], u_v, 1),
                 ("2A", 1, u_xtr, [("scalar", u_xcopy)], u_xtv, 1),
                 ("2C", -1, u_otr, [("scalar", u_ocopy)], u_otv, 1),
                 QK(0, "3A", 1),
                 ("3B", -1, project_out(OT1, a1_li1, u_otv, u_li), [("vector", add_out(u_li, r1, u_xo))], u_xo, 1),
                 QK(1, "3C", 1)]
        job_banks = [psum[:, 2, :], psum[:, 3, :], psum[:, 6, :]]
        NB = len(job_banks)
        turns1 = [Turns(B, [(d, counter, ev) for _, d, _, _, counter, ev in jobs1[n::NB]]) for n in range(NB)]
        rowsXA, rowsXO = (lambda b: XA[:, b, :]), (lambda b: XO[:, b, :])
        for g in range(4):
            at = lambda lag: (0 if g >= lag else -1, (g - lag) % 4)
            a1.add("vector", 0, G(u_max, g))
            a1.add("tensor", 0, G(u_scores, g))
            if g == 0:
                a1.add("gpsimd", 4, gather)
                a1.add("vector", 3, combine)
            d_, g_ = at(1)
            a1.add("vector", d_, G(u_mask, g_))
            for place in "ABC":
                if place == "B":
                    a1.add("scalar", 0, G(u_exp, g))
                    a1.add("tensor", d_, G(u_transpose, g_))
                if place == "C":
                    d, g2 = at(2)
                    a1.add("tensor", d, G(u_values, g2))
                for n, (where_, d, pe, copies, _, _) in enumerate(jobs1):
                    if where_ == f"{g}{place}":
                        def job1(b, n=n, pe=pe):
                            turns1[n % NB].wait_before(te, n // NB, b)
                            pe(b, job_banks[n % NB])
                        a1.add("tensor", d, job1)
                        for who, copy in copies:
                            a1.add(who, d, lambda b, n=n, copy=copy: copy(b, job_banks[n % NB]))
            if g == 0:
                nC.plan_apply(a1, 1, rowsXA, lambda b: xh1, lambda b: [(u_xt, b - 1, None)])
                nA.plan(a1, 2, rowsX, lambda b: [(c_cmb, b, None)])
            if g == 1:
                a1.add("vector", -1, u_recip)
                a1.add("vector", -1, u_divide)
                nA.plan_apply(a1, 2, rowsX, lambda b: y0, lambda b: [(nB.c_xh, b - 1, None)])
                nB.plan(a1, 2, lambda b: y0, lambda b: [(nA.c_xh, b, None)])
            if g == 2:
                nB.plan_apply(a1, 2, lambda b: y0, lambda b: xb1, lambda b: [(r1.xa, b - 1, 1)])
                a1.add("gpsimd", 2, lambda b: r1.affine(b, []))
            if g == 3:
                nD.plan(a1, -1, rowsXO, lambda b: [(u_xo, b, None)])
                nC.plan(a1, 2, rowsXA, lambda b: [(r1.xa, b, 2)])
                nD.plan_apply(a1, -1, rowsXO, lambda b: xh3, lambda b: [(u_ht, b - 1, None)])
                a1.add("gpsimd", -1, lambda b: r1.finish(b, nD))

        class FeedForward:
            def __init__(self, tag, w1, bias, w2, func, ready, add, follows=None):
                self.w1, self.bias, self.w2, self.func, self.ready, self.post = w1, bias, w2, func, ready, add
                self.pipe = Pipeline(B // GB)
                old = follows.counters if follows else [None] * 4
                self.counters = [Counter(nc, f"{tag}_{name}", per, 1, items, o) for (name, per, items), o in zip(
                    (("h", FB, B // GB), ("gl", FB, B // GB), ("y", GB, B // GB), ("done", 1, B)), old)]
                self.h, self.gl, self.y, self.done = self.counters

            def up(self, g, f):
                if f == 0:
                    wait(te, self.ready, g * GB + GB - 1)
                wait(te, self.gl, g, f + 1 - 4)
                for cb in range(CB):
                    ins = te.matmul(psS[:, f % 4, 0:GS], self.w1[:, cb, XH(f)], hT[:, cb, bass.ds(g * GS, GS)],
                                    start=cb == 0, stop=cb == CB - 1)
                ins.then_inc(self.h.sem, 1)

            def act(self, g, f):
                wait(ae, self.h, g, f + 1)
                if f == 0:
                    wait(ae, self.y, g - 1)
                if self.bias is None:
                    ins = ae.activation(hid[:, f, :], psS[:, f % 4, 0:GS], self.func)
                else:
                    ins = ae.activation(hid[:, f, :], psS[:, f % 4, 0:GS], self.func, bias=self.bias[:, f:f + 1])
                ins.then_inc(self.gl.sem, 1)

            def down(self, g, q):
                if q == 0:
                    wait(te, self.gl, g)
                wait(te, self.done, g * GB + q - 2)
                for f in range(FB):
                    ins = te.matmul(psT[0:S, q % 2, 0:C], hid[:, f, q * S:(q + 1) * S], self.w2[:, f, :],
                                    start=f == 0, stop=f == FB - 1)
                ins.then_inc(self.y.sem, 1)

            def add(self, g, q):
                wait(ve, self.y, g, q + 1)
                self.post(g * GB + q, psT[0:S, q % 2, 0:C]).then_inc(self.done.sem, 1)

            def plan(self, each=()):
                def extras(slot):
                    for slot_, who, d, action in each:
                        if slot_ == slot:
                            self.pipe.add(who, d, action)
                for f in range(2, FB + 2):
                    extras(f - 2)
                    d, f = (0, f) if f < FB else (1, f - FB)
                    self.pipe.add("tensor", d, lambda g, f=f: self.up(g, f))
                    if d == 0:
                        self.pipe.add("scalar", 0, lambda g, f=f: self.act(g, f))
                for q in range(GB):
                    self.pipe.add("tensor", 0, lambda g, q=q: self.down(g, q))
                    self.pipe.add("vector", 0, lambda g, q=q: self.add(g, q))
                    extras(FB + q)
                for f in range(2):
                    self.pipe.add("scalar", 1, lambda g, f=f: self.act(g, f))

        def add_f1(b, y):
            wait(ve, r1.fin, b)
            return ve.tensor_tensor(XO[:, b, :], y, XO[:, b, :], ALU.add)
        f_1 = FeedForward("f1", a1_li2, k["a1_li2_b"], a1_li3, ACT.Gelu, u_htv, add_f1)
        f_1.plan()

        a2 = Pipeline(B)
        x2 = Cross("a2", 32, wq2, wk2, wv2, k["mask1"], ctx_step=1, follows=x0)
        nE, nF, nG = (Norm(n, follows=old) for n, old in (("nE", nA), ("nF", nB), ("nG", nC)))
        nX = Norm("nX", LK, NK, follows=nD)
        xb2, xh4, xs2 = carve(wa1, (S, C), (S, C), (S, C))
        r2 = Residual("r2", nE, xb2, xs2, "ln2", "a2")
        s_cx = Counter(nc, "cx", 1, 16)
        v_li, v_xo, v_ht, v_htv, v_ct = (Counter(nc, "a2_" + n, follows=old) for n, old in (
            ("li", u_li), ("xo", u_xo), ("ht", u_ht), ("htv", u_htv), ("ct", u_xt)))

        def load_ctx(b):
            if isinstance(b, int) and b == 0:
                wait(se, f_1.y, 0, 1)
            wait(se, nX.c_xh, b - 1)
            se.dma_start(x2.cx, t["ctx"][b, :, :].rearrange("(n p) d -> p n d", p=LK)).then_inc(s_cx.sem, 16)

        def transpose_rows2(b):
            wait(te, nF.c_xh, b)
            transpose_blocks(x2.xh, CB, S).then_inc(x2.xt.sem, 1)

        def copy_rows2(b):
            wait(ae, x2.xt, b)
            for cb in range(CB):
                ins = affine_copy(x2.xT[:, cb, :], psM[:, cb * S:(cb + 1) * S], k["a2_lnx_g"], k["a2_lnx_b"], cb)
            ins.then_inc(x2.xtv.sem, 1)

        def transpose_ctx(b):
            wait(te, nX.c_xh, b)
            for kb in range(NK):
                ins = te.transpose(psM[:, kb * LK:(kb + 1) * LK], x2.cxh[:, kb, :], ident[0:LK, 0:LK])
            ins.then_inc(v_ct.sem, 1)

        def copy_ctx(b):
            wait(ae, v_ct, b)
            affine_copy(x2.ctxT, psM[:, 0:L], k["a2_lny_g"], k["a2_lny_b"], 0).then_inc(x2.ctx.sem, 1)

        Qj = lambda g, s_, d: (s_, d, J(x2.queries, g), "vector", J(x2.spread_queries, g), x2.q, g + 1)
        Kj = lambda g, s_, d: (s_, d, J(x2.keys, g), "scalar", J(x2.copy_keys, g), x2.kt, g + 1)
        Vj = lambda g, s_, d: (s_, d, J(x2.values, g), "vector", J(x2.copy_values, g), x2.v, g + 1)
        jobs2 = [Qj(2, 0, 0), Kj(2, 1, 0), Vj(2, 2, 0), Qj(3, 3, 0), Kj(3, 4, 0),
                 (5, 1, transpose_rows2, "scalar", copy_rows2, x2.xtv, 1),
                 Vj(3, 6, 0),
                 (7, 1, transpose_ctx, "scalar", copy_ctx, x2.ctx, 1),
                 (8, -1, x2.transpose_o, "scalar", x2.copy_o, x2.otv, 1),
                 (9, -1, project_out(x2.OT, a2_li1, x2.otv, v_li), "vector", add_out(v_li, r2, v_xo), v_xo, 1),
                 Kj(0, 10, 1), Vj(0, 11, 1), Qj(0, 12, 1), Qj(1, 13, 1),
                 (13, -1, transpose_h(nG, xh4, v_ht), "scalar", copy_h(v_ht, "a2", v_htv), v_htv, 1),
                 Kj(1, 14, 1), Vj(1, 15, 1)]
        extra2 = [(0, "vector", 1, lambda b: nE.bn_stats(b, XO[:, b, :], [(f_1.done, b, None)] if isinstance(b, int) else [])),
                  (0, "vector", 1, nE.bn_aggr), (0, "gpsimd", 1, nE.power),
                  (1, "vector", 1, lambda b: nX.bn_stats(b, x2.cx, [(s_cx, b, None)])),
                  (1, "vector", 1, nX.bn_aggr), (1, "gpsimd", 1, nX.power),
                  (1, "vector", 1, lambda b: nE.apply(b, XO[:, b, :], xb2, [(r2.xa, b - 1, 1)])),
                  (1, "gpsimd", 1, lambda b: r2.affine(b, [])),
                  (3, "vector", 1, lambda b: nF.bn_stats(b, XA[:, b, :], [(r2.xa, b, 2)])),
                  (3, "vector", 1, nF.bn_aggr), (3, "gpsimd", 1, nF.power),
                  (4, "vector", 1, lambda b: nF.apply(b, XA[:, b, :], x2.xh, [(x2.xt, b - 1, None)])),
                  (5, "vector", 1, lambda b: nX.apply(b, x2.cx, x2.cxh, [(v_ct, b - 1, None)])),
                  (9, "vector", -1, lambda b: nG.bn_stats(b, XO[:, b, :], [(v_xo, b, None)])),
                  (9, "vector", -1, nG.bn_aggr), (9, "gpsimd", -1, nG.power),
                  (11, "vector", -1, lambda b: nG.apply(b, XO[:, b, :], xh4, [(v_ht, b - 1, None)])),
                  (11, "gpsimd", -1, lambda b: r2.finish(b, nG))]
        a2.add("sync", 1, load_ctx)
        a2.add("tensor", 1, lambda b: once(b, [0]) and wait(te, s_wa2, 0))
        x2.plan(a2, jobs2, extra2)

        def add_f2(b, y):
            wait(ve, r2.fin, b)
            return ve.tensor_tensor(X[:, b, :], y, XO[:, b, :], ALU.add)
        f_2 = FeedForward("f2", a2_li2, k["a2_li2_b"], a2_li3, ACT.Gelu, v_htv, add_f2, f_1)
        nH = Norm("nH", follows=nE)
        g_t, g_tv, g_ta, g_l, g_lv = (Counter(nc, "g_" + n, follows=old) for n, old in (
            ("t", rt), ("tv", rtv), ("ta", u_rcp), ("l", rl), ("lv", rlv)))

        def transpose_g(b):
            wait(te, nH.c_xh, b)
            wait(te, g_tv, b - 1)
            transpose_blocks(xr, CB, S).then_inc(g_t.sem, 1)

        def copy_g_static(b):
            wait(ve, g_t, b)
            wait(ve, g_ta, b)
            wait(ve, g_l, b - 1)
            ve.tensor_copy(xTr, psum_rows(CB, S)).then_inc(g_tv.sem, 1)

        def copy_g(b):
            wait(ae, g_t, b)
            ae.activation(hT[:, :, bass.ds(b * S, S)], psum_rows(CB, S), ACT.Copy).then_inc(g_ta.sem, 1)

        def logits_g(b):
            wait(te, g_tv, b)
            wait(te, g_lv, b - 1)
            for cb in range(CB):
                ins = te.matmul(psO[0:S, 0:E], xTr[:, cb, :], wg[:, cb, :], start=cb == 0, stop=cb == CB - 1)
            ins.then_inc(g_l.sem, 1)

        def copy_logits_g(b):
            wait(ve, g_l, b)
            ve.tensor_copy(LG[:, b, :], psO[0:S, 0:E]).then_inc(g_lv.sem, 1)
        of = lambda q, f: (lambda g: f(g * GB + q))
        router = [part for q in range(GB) for part in (
            (2 * q, "vector", -1, of(q, lambda b: nH.bn_stats(b, X[:, b, :], [(f_2.done, b, None)]))),
            (2 * q, "vector", -1, of(q, nH.bn_aggr)), (2 * q, "gpsimd", -1, of(q, nH.power)),
            (2 * q + 1, "vector", -1, of(q, lambda b: nH.apply(b, X[:, b, :], xr, [(g_t, b - 1, None)]))),
            (2 * q + 2, "tensor", -1, of(q, transpose_g)), (2 * q + 2, "scalar", -1, of(q, copy_g)),
            (2 * q + 3, "vector", -1, of(q, copy_g_static)),
            (2 * q + 4, "tensor", -1, of(q, logits_g)), (2 * q + 5, "vector", -1, of(q, copy_logits_g)))]
        f_2.plan(router)

        gate_w = sb("gate_w", [S, B])
        c_gd, c_ge = Counter(nc, "gd"), Counter(nc, "ge")
        gchain = Chain("gating", ve)
        g_e, = carve(work[:, 8000:9000], (S, B, E))
        g_den, g_1, g_2 = carve(work[:, 9000:10000], *[(S, B)] * 3)

        def gating_vector():
            def step(ins):
                gchain(ins)
                gchain.settle()
            wait(ve, g_lv, B - 1)
            top_two(step)
            ve.tensor_tensor(g_e, LG[:, :, :], over_e(m1), ALU.subtract).then_inc(c_gd.sem, 1)
            ve.wait_ge(c_ge.sem, 1)
            step(ve.tensor_reduce(g_den, g_e, AX.X, ALU.add))
            step(ve.reciprocal(g_den, g_den))
            step(ve.tensor_tensor(g_e, g_e, over_e(g_den), ALU.mult))
            for oh, dst in ((oh1, g_1), (oh2, g_2)):
                step(ve.tensor_tensor(prod, oh, g_e, ALU.mult))
                step(ve.tensor_reduce(dst, prod, AX.X, ALU.add))
            step(ve.tensor_tensor(g_den, g_1, g_2, ALU.add))
            step(ve.tensor_scalar(g_den, g_den, float(np.finfo(np.float32).eps), None, ALU.max))
            step(ve.reciprocal(g_den, g_den))
            step(ve.tensor_tensor(g_1, g_1, g_den, ALU.mult))
            step(ve.tensor_tensor(g_2, g_2, g_den, ALU.mult))
            step(ve.tensor_tensor(gate_w[:, :], g_1, g_2, ALU.add))

        def gating_scalar():
            ae.wait_ge(c_gd.sem, 1)
            ae.activation(g_e, g_e, ACT.Exp).then_inc(c_ge.sem, 1)

        def add_f3(b, y):
            return ve.scalar_tensor_tensor(X[:, b, :], y, gate_w[:, bass.ds(b, 1)], X[:, b, :], ALU.mult, ALU.add)
        f_3 = FeedForward("f3", f1w, None, f2w, ACT.Relu, g_ta, add_f3, f_2)

        def store(b):
            wait(se, f_3.done, b)
            se.dma_start(out[b, :, :], X[:, b, :]).then_inc(s_out.sem, 16)
        f_3.plan([(FB + q, "sync", 0, of(q, store)) for q in range(GB)]
                 + [(4, "scalar", 0, lambda g: once(g, [0]) and gating_scalar())])

        def layer1_sync(eng, dma, blocks):
            wait(eng, m_yg, TILES - 1)
            for n, dst in (("a2_wq", wq2), ("a2_wk", wk2), ("a2_wv", wv2), ("a2_li1", a2_li1), ("a2_li2", a2_li2),
                           ("a2_li3", a2_li3), ("f1", f1w), ("f2", f2w), ("wg", wg[:, :, :])):
                dma(dst, blocks(t[n]), s_wa2)
            a2.run("sync", eng)
            if stop >= 4:
                f_3.pipe.run("sync", eng)
                wait(eng, s_out, 0)

        def layer1(name, eng):
            if name == "tensor":
                wait(eng, s_wa1, 0)
            a1.run(name, eng)
            f_1.pipe.run(name, eng)
            a2.run(name, eng)
            f_2.pipe.run(name, eng)
            if stop >= 4:
                if name == "vector":
                    gating_vector()
                f_3.pipe.run(name, eng)
        with nc.Block() as block:
            @block.sync
            def _(eng):
                dma = lambda dst, src, c_: eng.dma_start(dst, src).then_inc(c_.sem, 16)
                blocks = lambda w: w.rearrange("(n p) m -> p n m", p=P)
                dma(X[:, 0:1, :], t["x"][0:1, :, :].rearrange("b s c -> s b c"), s_x)
                dma(const[:, :], t["const"], s_const)
                dma(cols[:, :], t["cols"], s_const)
                dma(wq0, blocks(t["wq0"]), s_w0)
                dma(wk0[:, 0, :], t["wkv0"][:, 0:C], s_w0)
                dma(wv0[:, 0, :], t["wkv0"][:, C:2 * C], s_w0)
                dma(wo0, blocks(t["wo0"]), s_w0)
                x0_first(eng, dma, blocks)
                a0.run("sync", eng)
                wait(eng, c_xs, B - 1)
                wait(eng, rlv, B - 1)
                for n, name in enumerate(ROWS):
                    dma(rows[name], t["rows"][n, :].partition_broadcast(S), s_rows)
                for n, dst in (("wq", wq1), ("wk", wk1), ("wv", wv1), ("li1", a1_li1), ("li2", a1_li2), ("li3", a1_li3)):
                    dma(dst, blocks(t["a1_" + n]), s_wa1)
                if stop >= 2:
                    tiles.run("sync", eng)
                if stop >= 3:
                    layer1_sync(eng, dma, blocks)
                if stop < 4:
                    wait(eng, res0, B - 1)
                    if stop >= 2:
                        wait(eng, c_cmb, B - 1)
                    if stop >= 3:
                        wait(eng, f_2.done, B - 1)
                    eng.dma_start(out.rearrange("b s c -> s b c"), X[:, :, :]).then_inc(s_out.sem, 16)
                    eng.wait_ge(s_out.sem, 16)

            @block.tensor
            def _(eng):
                wait(eng, s_const, 0)
                a0.run("tensor", eng)
                if stop >= 2:
                    route_tensor()
                    tiles_ready(eng)
                    tiles.run("tensor", eng)
                if stop >= 3:
                    layer1("tensor", eng)

            @block.scalar
            def _(eng):
                wait(eng, s_const, 0)
                a0.run("scalar", eng)
                if stop >= 2:
                    route_scalar()
                    tiles.run("scalar", eng)
                if stop >= 3:
                    layer1("scalar", eng)

            @block.vector
            def _(eng):
                ve.memset(yk_zero, 0.0).then_inc(c_zero.sem, 1)
                wait(eng, s_const, 0)
                a0.run("vector", eng)
                if stop >= 2:
                    route_vector()
                    tiles.run("vector", eng)
                if stop >= 3:
                    layer1("vector", eng)

            @block.gpsimd
            def _(eng):
                wait(eng, s_const, 0)
                a0.run("gpsimd", eng)
                if stop >= 2:
                    scatter()
                if stop >= 3:
                    layer1("gpsimd", eng)


def layout(i):
    a = {n: np.asarray(v) for n, v in i.items()}
    T = lambda x, *axes: np.ascontiguousarray(np.transpose(x, axes) if axes else x.T)
    g = {n[9:]: v for n, v in a.items() if n.startswith("L1_xattn_")}
    cols = np.concatenate([T(g[n].reshape(w, P)) for n, w in COLS], 1)
    heads = lambda w: T(w, 1, 0, 2).reshape(w.shape[1], H * w.shape[2])
    d = dict(x=a["x"], const=CONST, cols=cols, rows=np.stack([g[n] for n in ROWS]),
             ctx=a["ctx_512"], ctxT=T(a["ctx_512"], 0, 2, 1),
             wq0=T(a["L0_xattn_Wq"]), wkv0=T(a["L0_xattn_Wkv"]), wo0=T(a["L0_xattn_Wo"]),
             rw=T(a["L0_ffn_router_w"]), w1e=T(a["L0_ffn_w1"], 0, 2, 1), w2e=T(a["L0_ffn_w2"], 0, 2, 1),
             b1e=a["L0_ffn_b1"], b2e=a["L0_ffn_b2"],
             wg=a["L1_ffn_Wg"], f1=a["L1_ffn_w1"], f2=a["L1_ffn_w2"])
    for p in ("a1", "a2"):
        for n in ("wq", "wk", "wv"):
            d[f"{p}_{n}"] = heads(g[f"{p}_{n}"])
        for n in ("li1", "li2", "li3"):
            d[f"{p}_{n}"] = g[f"{p}_{n}_w"]
    return d


def kernel(**inputs):
    import concourse.bacc as bacc
    from concourse.bass_utils import run_bass_kernel_spmd

    nc = bacc.Bacc("TRN2", target_bir_lowering=False, num_devices=1)
    arrays = {f"in_{n}": np.ascontiguousarray(v) for n, v in layout(inputs).items()}
    t = {n[3:]: nc.dram_tensor(n, v.shape, mybir.dt.from_np(v.dtype), kind="ExternalInput").ap()
         for n, v in arrays.items()}
    for n in ("slots_x", "slots_y"):
        t[n] = nc.dram_tensor(n, (TILES * P, C), F32, kind="Internal").ap()
    out = nc.dram_tensor("out", (B, S, C), F32, kind="ExternalOutput").ap()
    program(nc, t, out)
    return run_bass_kernel_spmd(nc, [arrays], core_ids=[0]).results[0]["out"]
```

```python
from contextlib import ExitStack

import numpy as np

import concourse.bass as bass
from concourse import mybir
from concourse.alu_op_type import AluOpType as ALU

F32 = mybir.dt.float32
U32 = mybir.dt.uint32
ACT = mybir.ActivationFunctionType
AX = mybir.AxisListType

P = 128
B, S, C = 16, 112, 256
L, D = 375, 128
LK = 125
NK = L // LK
CB = C // P
H = 16
EPS = 1e-5


class Counter:

    def __init__(self, nc, name, per=1, step=1, items=B, follows=None):
        self.sem = follows.sem if follows else nc.alloc_semaphore(name)
        self.base = follows.base + follows.items * follows.per * follows.step if follows else 0
        self.per, self.step, self.items = per, step, items

    def after(self, item, k=None):
        return item * (self.per * self.step) + (self.base + (self.per if k is None else k) * self.step)


def wait(eng, counter, item, k=None):
    value = counter.after(item, k)
    if isinstance(value, int) and value <= counter.base:
        return
    eng.wait_ge(counter.sem, value)


class Pipeline:

    def __init__(self, items):
        self.items, self.actions = items, {}
        self.peel = 0

    def add(self, engine, distance, action):
        self.actions.setdefault(engine, []).append((distance, action))

    def run(self, name, eng):
        todo = self.actions.get(name, [])
        if not todo:
            return
        ahead = max(0, max(d for d, _ in todo))
        behind = max(0, max(-d for d, _ in todo))

        def iteration(it):
            for d, action in todo:
                if not isinstance(it, int) or 0 <= it + d < self.items:
                    action(it + d)

        first, last = behind + 1, self.items - max(ahead, self.peel)
        if last - first < 2:
            first = last = self.items
        for it in range(-ahead, first):
            iteration(it)
        if last > first:
            with eng.Fori(first, last) as it:
                iteration(it)
        for it in range(last, self.items + behind):
            iteration(it)


class Turns:

    def __init__(self, items, jobs):
        self.items, self.jobs = items, jobs

    def wait_before(self, eng, index, item):
        it = item - self.jobs[index][0]
        for back in range(1, 2 * len(self.jobs) + 1):
            wrap, at = divmod(index - back, len(self.jobs))
            distance, counter, k = self.jobs[at]
            other = it + distance if wrap == 0 else it + (wrap + distance)
            if not isinstance(it, int) or 0 <= other < self.items:
                wait(eng, counter, other, k)
                return



def constants():
    p = np.arange(P)
    parts = dict(
        ident=np.eye(P), ones=np.ones((P, P)),
        mask0=(p[:, None] // 16 == np.arange(8)[None, :]) * (16.0 ** -0.5),
        mask1=(p[:, None] // 32 == np.arange(4)[None, :]) * (32.0 ** -0.5),
        before=(p[:, None] < p[None, :]) * 1.0,
        after=(p[:, None] > p[None, :S]) * 1.0,
        powm=np.full((P, 1), -0.5), eps=np.full((P, 1), EPS),
        iota=np.tile(np.arange(40.0), (P, 1)),
        down=np.tile(E - np.arange(float(E)), (P, 1)),
        region=np.tile(float(ROOM) * np.arange(E), (P, 1)),
        steps=np.tile(float(P) * np.arange(B * S // P), (P, 1)))
    at, where = 0, {}
    for n, a in parts.items():
        where[n] = (at, at + a.shape[1])
        at += a.shape[1]
    return where, np.concatenate(list(parts.values()), 1).astype(np.float32)


E, F0, TOP = 8, 512, 2
TILES = B * S * TOP // P + E - 1
ROOM = B * S + P
IDLE = TILES - B * S * TOP // P
SLOTS = E * ROOM + IDLE * P
UNROLL = 5
assert TILES % UNROLL == 0
F1 = 1024
FB = F1 // P
GB = 4
GS = GB * S
CONST_AT, CONST = constants()

COLS = [("a1_lnx_g", 2), ("a1_lnx_b", 2), ("a1_lny_g", 2), ("a1_lny_b", 2), ("a1_ln3_g", 2), ("a1_ln3_b", 2),
        ("a1_li2_b", 8), ("a2_lnx_g", 2), ("a2_lnx_b", 2), ("a2_lny_g", 1), ("a2_lny_b", 1), ("a2_ln3_g", 2),
        ("a2_ln3_b", 2), ("a2_li2_b", 8)]
ROWS = ["ln1_g", "ln1_b", "ln2_g", "ln2_b", "a1_li1_b", "a1_li3_b", "a2_li1_b", "a2_li3_b"]


def carve(region, *shapes):
    at, out = 0, []
    for parts, *free in shapes:
        n = int(np.prod(free))
        assert at + n <= region.shape[1], (at, n)
        v = region[0:parts, at:at + n]
        if len(free) == 2:
            v = v.rearrange("p (a b) -> p a b", a=free[0])
        elif len(free) == 3:
            v = v.rearrange("p (a b c) -> p a b c", a=free[0], b=free[1])
        out.append(v)
        at += n
    return out


def program(nc, t, out):
    te, ve, ae, ge, se = nc.tensor, nc.vector, nc.scalar, nc.gpsimd, nc.sync
    with ExitStack() as ctx:
        def sb(name, shape, dt=F32):
            return ctx.enter_context(nc.sbuf_tensor(name, shape, dt))

        X = sb("X", [S, B, C])
        const = sb("const", [P, CONST.shape[1]])
        k = {n: const[:, a:b] for n, (a, b) in CONST_AT.items()}
        ident = k["ident"]
        cols = sb("cols", [P, sum(n for _, n in COLS)])
        at = 0
        for n, w in COLS:
            k[n] = cols[:, at:at + w]
            at += w
        junk, junk2 = sb("junk", [1, 64]), sb("junk2", [1, 64])
        turn = dict(vector=0, gpsimd=0)

        def word(name):
            turn[name] = (turn[name] + 1) % 64
            return slice(turn[name], turn[name] + 1)
        sums = sb("sums", [S, B * H])
        rsum = sb("rsum", [S, H])
        nmax = sb("nmax", [S, H])
        LG = sb("LG", [S, B, E])
        p12 = sb("p12", [S, 2, B])

        first = sb("first", [P, 2048])
        work = sb("work", [P, 10260])
        arena = sb("arena", [P, 26624])
        wa1 = sb("wa1", [P, 8192])
        wq0, wk0, wv0, wo0 = carve(first, (P, CB, C), (P, 1, C), (P, 1, C), (P, CB, C))
        rows = dict(zip(ROWS, carve(first, *[(S, C)] * len(ROWS))))
        w1e, w2e, b1e, b2e, zeros = carve(arena, (P, E, CB, F0), (P, E, F0 // P, C), (P, E, F0), (P, E, C), (P, IDLE, C))
        psum = ctx.enter_context(nc.psum_tensor("psum", [P, 8, 512], F32))
        psS, psT, psM, psO = psum[:, 0:4, :], psum[:, 4:6, :], psum[:, 6, :], psum[:, 7, :]

        s_const, s_x, s_w0 = Counter(nc, "const", 2, 16), Counter(nc, "x", 1, 16), Counter(nc, "w0", 5, 16)
        s_out = Counter(nc, "out", B, 16)

        s_x1 = Counter(nc, "x1", 1, 16)
        c_zero, c_fill, c_tails = Counter(nc, "zero"), Counter(nc, "fill", 1, 16), Counter(nc, "tails", E, 16)
        s_we = Counter(nc, "we", 2 + 2 * B, 16)

        def gate(waits):
            for counter, item, k_ in waits:
                wait(ve, counter, item, k_)
            ve.memset(junk[:, word("vector")], 0.0)

        def pool_gate(*waits):
            for counter, item, k_ in waits:
                wait(ge, counter, item, k_)
            ge.tensor_tensor(junk2[:, word("gpsimd")], k["eps"][0:1, :], k["eps"][0:1, :], ALU.add)

        class Norm:

            def __init__(self, tag, rows_=S, blocks=1, follows=None):
                self.rows, self.blocks = rows_, blocks
                self.buf = sb(tag + "_stat", [rows_, blocks * 10])
                b = self.buf
                self.sixes = b[:, 0:6 * blocks].rearrange("p (n s) -> p n s", n=blocks)
                self.mv = b[:, 6 * blocks:8 * blocks].rearrange("p (n s) -> p n s", n=blocks)
                self.veps, self.rstd = b[:, 8 * blocks:9 * blocks], b[:, 9 * blocks:10 * blocks]
                c = lambda name, per=1: Counter(nc, tag + "_" + name, per,
                                                follows=follows and follows.counters[name])
                self.counters = dict(bn=c("bn"), mv=c("mv"), rs=c("rs", 2), xh=c("xh"))
                self.c_bn, self.c_mv, self.c_rs, self.c_xh = self.counters.values()

            def bn_stats(self, b, src, ready):
                gate(ready + [(self.c_mv, b - 1, None)])
                for n in range(self.blocks):
                    ins = ve.bn_stats(self.sixes[:, n, :], src[:, n, :] if self.blocks > 1 else src)
                ins.then_inc(self.c_bn.sem, 1)

            def bn_aggr(self, b):
                gate([(self.c_bn, b, None), (self.c_rs, b - 1, None), (self.c_xh, b - 1, None)])
                for n in range(self.blocks):
                    ins = ve.bn_aggr(self.mv[:, n, :], self.sixes[:, n, :])
                ins.then_inc(self.c_mv.sem, 1)

            def power(self, b):
                r, n = self.rows, self.blocks
                wait(ge, self.c_mv, b)
                ge.tensor_tensor(self.veps, self.mv[:, :, 1], k["eps"][0:r, :].broadcast_to([r, n]),
                                 ALU.add).then_inc(self.c_rs.sem, 1)
                wait(ge, self.c_rs, b, 1)
                wait(ge, self.c_xh, b - 1)
                ge.tensor_tensor(self.rstd, self.veps, k["powm"][0:r, :].broadcast_to([r, n]),
                                 ALU.pow).then_inc(self.c_rs.sem, 1)

            def apply(self, b, src, dst, free):
                wait(ve, self.c_rs, b)
                for counter, item, k_ in free:
                    wait(ve, counter, item, k_)
                for n in range(self.blocks):
                    a, d = (src[:, n, :], dst[:, n, :]) if self.blocks > 1 else (src, dst)
                    ins = ve.tensor_scalar(d, a, self.mv[:, n, 0:1], self.rstd[:, n:n + 1],
                                           ALU.subtract, ALU.mult)
                ins.then_inc(self.c_xh.sem, 1)

            def plan(self, pipe, distance, src, ready):
                pipe.add("vector", distance, lambda b: self.bn_stats(b, src(b), ready(b)))
                pipe.add("vector", distance, lambda b: self.bn_aggr(b))
                pipe.add("gpsimd", distance, lambda b: self.power(b))

            def plan_apply(self, pipe, distance, src, dst, free):
                pipe.add("vector", distance, lambda b: self.apply(b, src(b), dst(b), free(b)))

        def once(b, waits):
            return waits if isinstance(b, int) and b == 0 else []

        def transpose_blocks(src, n, rows_, bank=None):
            bank = psM if bank is None else bank
            for cb in range(n):
                ins = te.transpose(bank[:, cb * rows_:(cb + 1) * rows_], src[:, cb * P:(cb + 1) * P],
                                   ident[0:rows_, 0:rows_])
            return ins

        def psum_rows(n, width, bank=None):
            return (psM if bank is None else bank)[:, 0:n * width].rearrange("p (n w) -> p n w", n=n)

        class Cross:
            def __init__(self, tag, dh, wq, wk, wv, mask, ctx_step=16, follows=None):
                self.tag, self.dh, self.wq, self.wk, self.wv, self.mask = tag, dh, wq, wk, wv, mask
                self.G = P // dh
                self.chunks = H // self.G
                HD = H * dh
                (self.Qb, self.KT, self.V, self.Pr, self.PT, self.xh, self.xT, self.On, self.OT, self.ctxT,
                 self.cx, self.cxh) = carve(
                    work, (P, self.chunks, self.G, S), (P, self.chunks, L), (LK, NK, HD), (S, 4, L), (LK, 4, NK * S),
                    (S, C), (P, CB, S), (S, HD), (P, HD // P, S), (P, L), (LK, NK, D), (LK, NK, D))
                n = self.chunks
                self.counters = {}

                def c(name, per=1, step=1):
                    old = follows.counters[name] if follows and name in follows.counters else None
                    self.counters[name] = Counter(nc, tag + "_" + name, per, step, follows=old)
                    return self.counters[name]
                self.c = c
                self.BY_ACT = [1, 3, 6, 9, 12, 15]
                self.ctx = c("ctx", 1, ctx_step)
                self.xt, self.xtv = c("xt"), c("xtv")
                self.qp, self.q, self.kp, self.kt, self.vp, self.v = (c(x, n) for x in ("qp", "q", "kp", "kt", "vp", "v"))
                self.s, self.mx, self.e = c("s", H), c("mx", H // 2), c("e", H)
                self.tr, self.pv = c("tr", H), c("pv", H)
                self.pta, self.ptv = c("pta", len(self.BY_ACT)), c("ptv", H - len(self.BY_ACT))
                self.rcp, self.on, self.ot, self.otv = c("rcp"), c("on"), c("ot"), c("otv")

            def pt_copied(self, eng, b, h):
                if h < 0:
                    b, h = b - 1, h + H
                if h in self.BY_ACT:
                    wait(eng, self.pta, b, self.BY_ACT.index(h) + 1)
                else:
                    wait(eng, self.ptv, b, h + 1 - sum(x < h for x in self.BY_ACT))

            def scores(self, b, h):
                c, g = divmod(h, self.G)
                if g == 0:
                    wait(te, self.q, b, c + 1)
                    wait(te, self.kt, b, c + 1)
                wait(te, self.e, b, h + 1 - 4)
                te.matmul(psS[0:S, h % 4, 0:L], self.Qb[:, c, g, :], self.KT[:, c, :],
                          start=True, stop=True).then_inc(self.s.sem, 1)

            def row_max(self, b, pair):
                h = 2 * pair
                wait(ve, self.s, b, h + 2)
                ve.tensor_reduce(nmax[:, h:h + 2], psS[0:S, h % 4:h % 4 + 2, 0:L],
                                 AX.X, ALU.max, negate=True).then_inc(self.mx.sem, 1)

            def numerators(self, b, h):
                if h % 2 == 0:
                    wait(ae, self.mx, b, h // 2 + 1)
                wait(ae, self.tr, b, h + 1 - 4)
                ae.activation(self.Pr[:, h % 4, :], psS[0:S, h % 4, 0:L], ACT.Exp, bias=nmax[:, h:h + 1],
                              accum_out=sums[:, bass.ds(b * H + h, 1)]).then_inc(self.e.sem, 1)

            def transpose_numerators(self, b, h):
                wait(te, self.e, b, h + 1)
                self.pt_copied(te, b, h - 2)
                for kb in range(NK):
                    ins = te.transpose(psT[0:LK, h % 2, kb * S:(kb + 1) * S],
                                       self.Pr[:, h % 4, kb * LK:(kb + 1) * LK], ident[0:S, 0:S])
                ins.then_inc(self.tr.sem, 1)

            def copy_transposed(self, b, h):
                eng = ae if h in self.BY_ACT else ve
                wait(eng, self.tr, b, h + 1)
                wait(eng, self.pv, b, h + 1 - 4)
                dst, src = self.PT[:, h % 4, :], psT[0:LK, h % 2, 0:NK * S]
                if eng is ae:
                    ae.activation(dst, src, ACT.Copy).then_inc(self.pta.sem, 1)
                else:
                    ve.tensor_copy(dst, src).then_inc(self.ptv.sem, 1)

            def weigh_values(self, b, h):
                dh = self.dh
                self.pt_copied(te, b, h)
                if h % self.G == 0:
                    wait(te, self.v, b, h // self.G + 1)
                if h == 0:
                    wait(te, self.on, b - 1)
                for kb in range(NK):
                    ins = te.matmul(psO[0:S, h * dh:(h + 1) * dh], self.PT[:, h % 4, kb * S:(kb + 1) * S],
                                    self.V[:, kb, h * dh:(h + 1) * dh], start=kb == 0, stop=kb == NK - 1)
                ins.then_inc(self.pv.sem, 1)

            def queries(self, b, c):
                wait(te, self.xtv, b)
                for cb in range(CB):
                    ins = te.matmul(psM[:, 0:S], self.wq[:, cb, c * P:(c + 1) * P], self.xT[:, cb, :],
                                    start=cb == 0, stop=cb == CB - 1)
                ins.then_inc(self.qp.sem, 1)

            def spread_queries(self, b, c):
                wait(ve, self.qp, b, c + 1)
                wait(ve, self.s, b - 1, self.G * (c + 1))
                ve.tensor_tensor(self.Qb[:, c, :, :], psM[:, 0:S].unsqueeze(1).broadcast_to([P, self.G, S]),
                                 self.mask.unsqueeze(2).broadcast_to([P, self.G, S]), ALU.mult).then_inc(self.q.sem, 1)

            def keys(self, b, c):
                wait(te, self.ctx, b)
                te.matmul(psM[:, 0:L], self.wk[:, 0, c * P:(c + 1) * P], self.ctxT, start=True, stop=True)\
                  .then_inc(self.kp.sem, 1)

            def copy_keys(self, b, c):
                wait(ae, self.kp, b, c + 1)
                wait(ae, self.s, b - 1, self.G * (c + 1))
                ae.activation(self.KT[:, c, :], psM[:, 0:L], ACT.Copy).then_inc(self.kt.sem, 1)

            def values(self, b, c):
                for kb in range(NK):
                    ins = te.matmul(psM[0:LK, kb * P:(kb + 1) * P], self.ctxT[:, kb * LK:(kb + 1) * LK],
                                    self.wv[:, 0, c * P:(c + 1) * P], start=True, stop=True)
                ins.then_inc(self.vp.sem, 1)

            def copy_values(self, b, c):
                wait(ve, self.vp, b, c + 1)
                wait(ve, self.pv, b - 1, self.G * (c + 1))
                ve.tensor_copy(self.V[:, :, c * P:(c + 1) * P],
                               psM[0:LK, 0:NK * P].rearrange("p (n m) -> p n m", n=NK)).then_inc(self.v.sem, 1)

            def transpose_o(self, b):
                wait(te, self.on, b)
                transpose_blocks(self.On, H * self.dh // P, S).then_inc(self.ot.sem, 1)

            def copy_o(self, b):
                wait(ae, self.ot, b)
                n = H * self.dh // P
                ae.activation(self.OT[:, :, :], psM[:, 0:n * S], ACT.Copy).then_inc(self.otv.sem, 1)

            def recip_sums(self, b):
                wait(ve, self.e, b)
                wait(ve, self.on, b - 1)
                ve.reciprocal(rsum[:, :], sums[:, bass.ds(b * H, H)]).then_inc(self.rcp.sem, 1)

            def divide(self, b):
                wait(ve, self.rcp, b)
                wait(ve, self.pv, b)
                wait(ve, self.ot, b - 1)
                n = H * self.dh
                ve.tensor_tensor(self.On.rearrange("p (h d) -> p h d", h=H),
                                 psO[0:S, 0:n].rearrange("p (h d) -> p h d", h=H),
                                 rsum[:, :].unsqueeze(2).broadcast_to([S, H, self.dh]), ALU.mult).then_inc(self.on.sem, 1)

            def plan(self, pipe, jobs, extra, LT=4, LP=6):
                turns = Turns(B, [(d, counter, ev) for _, d, _, _, _, counter, ev in jobs])
                for h in range(H):
                    at = lambda lag: (0 if h >= lag else -1, (h - lag) % H)
                    dt, ht = at(LT)
                    dp, hp = at(LP)
                    pipe.add("tensor", 0, lambda b, h=h: self.scores(b, h))
                    if h % 2 == 1:
                        pipe.add("vector", 0, lambda b, h=h: self.row_max(b, h // 2))
                    pipe.add("tensor", dt, lambda b, g=ht: self.transpose_numerators(b, g))
                    if h == 5:
                        pipe.add("vector", -1, self.recip_sums)
                        pipe.add("vector", -1, self.divide)
                    for n, (step, d, pe, who, copy, counter, ev) in enumerate(jobs):
                        if step == h:
                            def job(b, n=n, pe=pe):
                                turns.wait_before(te, n, b)
                                pe(b)
                            pipe.add("tensor", d, job)
                            pipe.add(who, d, copy)
                    if h % 2 == 1:
                        pipe.add("scalar", 0, lambda b, h=h: self.numerators(b, h - 1))
                        pipe.add("scalar", 0, lambda b, h=h: self.numerators(b, h))
                    pipe.add("scalar" if ht in self.BY_ACT else "vector", dt, lambda b, g=ht: self.copy_transposed(b, g))
                    pipe.add("tensor", dp, lambda b, g=hp: self.weigh_values(b, g))
                    for step, who, d, action in extra:
                        if step == h:
                            pipe.add(who, d, action)

        a0 = Pipeline(B)
        x0 = Cross("a0", 16, wq0, wk0, wv0, k["mask0"])
        wo_p, res0 = x0.c("wo"), x0.c("res")
        n0, nr = Norm("n0"), Norm("nr")
        xr, xTr = carve(wa1[:, 1024:1536], (S, C), (P, CB, S))
        rw = sb("rw", [P, CB, E])
        rt, rtv, rl, rlv = x0.c("rt"), x0.c("rtv"), x0.c("rl"), x0.c("rlv")

        def load_ctxT(b):
            wait(se, x0.vp, b - 1)
            se.dma_start(x0.ctxT, t["ctxT"][b, :, :]).then_inc(x0.ctx.sem, 16)

        def transpose_rows0(b):
            wait(te, n0.c_xh, b)
            transpose_blocks(x0.xh, CB, S).then_inc(x0.xt.sem, 1)

        def copy_rows0(b):
            wait(ae, x0.xt, b)
            ae.activation(x0.xT, psum_rows(CB, S), ACT.Copy).then_inc(x0.xtv.sem, 1)

        def project_o0(b):
            wait(te, x0.otv, b)
            for cb in range(CB):
                ins = te.matmul(psM[0:S, 0:C], x0.OT[:, cb, :], wo0[:, cb, :], start=cb == 0, stop=cb == CB - 1)
            ins.then_inc(wo_p.sem, 1)

        def add_residual0(b):
            wait(ve, wo_p, b)
            ve.tensor_tensor(X[:, b, :], psM[0:S, 0:C], X[:, b, :], ALU.add).then_inc(res0.sem, 1)

        def copy_router(b):
            wait(ae, rt, b)
            wait(ae, rl, b - 1)
            ae.activation(xTr, psum_rows(CB, S), ACT.Copy).then_inc(rtv.sem, 1)

        def logits0(b):
            wait(te, rtv, b)
            for cb in range(CB):
                ins = te.matmul(psM[0:S, 0:E], xTr[:, cb, :], rw[:, cb, :], start=cb == 0, stop=cb == CB - 1)
            ins.then_inc(rl.sem, 1)

        def copy_logits0(b):
            wait(ve, rl, b)
            ve.tensor_copy(lg, psM[0:S, 0:E]).then_inc(rlv.sem, 1)

        lg, m_1, cand0, cm0, lg_2, m_2, chosen, both, pos0, next_slot, prod0, posk0 = carve(
            LG[:, :, :].rearrange("s b e -> s (b e)"), (S, E), (S, 1), (S, E), (S, 1), (S, E), (S, 1), (S, E),
            (S, TOP, E), (S, E), (S, E), (S, TOP, E), (S, TOP))
        slot = sb("slot", [S, TOP, B])
        idx_all = sb("idx", [S, TOP, B], U32)
        idx_b = sb("idx_b", [S, TOP, 1], U32)
        slots_x, slots_y = t["slots_x"], t["slots_y"]
        (xs0,) = carve(wa1[:, 1536:1792], (S, C))
        c_xs, c_rank = Counter(nc, "xs"), Counter(nc, "rank")
        c_pick, c_slot = Counter(nc, "pick", 11), Counter(nc, "slot", 6)
        c_sc = Counter(nc, "scatter", TOP, 16)

        def keep_rows(b):
            pool_gate((nr.c_xh, b, None), (c_sc, b - 1, None))
            ge.tensor_copy(xs0, xr).then_inc(c_xs.sem, 1)

        def pick(b, which):
            def step(n, ins):
                ins.then_inc(c_pick.sem, 1)
                wait(ve, c_pick, b, n)
            m, src = ((m_1, lg), (m_2, lg_2))[which]
            n = 5 * which
            if which == 0:
                wait(ve, rlv, b)
                wait(ve, c_slot, b - 1)
            step(n + 1, ve.tensor_reduce(m, src, AX.X, ALU.max))
            step(n + 2, ve.scalar_tensor_tensor(cand0, src, m, k["down"][0:S, :], ALU.is_equal, ALU.mult))
            step(n + 3, ve.tensor_reduce(cm0, cand0, AX.X, ALU.max))
            step(n + 4, ve.tensor_tensor(both[:, which, :], cand0, cm0.broadcast_to([S, E]), ALU.is_equal))
            if which == 0:
                step(n + 5, ve.scalar_tensor_tensor(lg_2, both[:, 0, :], -3.0e38, lg, ALU.mult, ALU.add))
            else:
                step(n + 5, ve.tensor_tensor(chosen, both[:, 0, :], both[:, 1, :], ALU.add))
                ve.tensor_tensor(p12[:, 1, bass.ds(b, 1)], m_2, m_1, ALU.subtract).then_inc(c_pick.sem, 1)

        def rank(b):
            wait(te, c_pick, b, 10)
            te.matmul(psM[0:S, 0:E], k["before"][0:S, 0:S], chosen, start=True, stop=True)
            te.matmul(psM[0:S, E:2 * E], k["ones"][0:S, 0:S], chosen, start=True, stop=True).then_inc(c_rank.sem, 1)

        def assign_slots(b):
            def step(n, ins):
                ins.then_inc(c_slot.sem, 1)
                wait(ve, c_slot, b, n)
            wait(ve, c_rank, b)
            step(1, ve.tensor_tensor(pos0, psM[0:S, 0:E], next_slot, ALU.add))
            step(2, ve.tensor_tensor(next_slot, psM[0:S, E:2 * E], next_slot, ALU.add))
            step(3, ve.tensor_tensor(prod0, both, pos0.unsqueeze(1).broadcast_to([S, TOP, E]), ALU.mult))
            step(4, ve.tensor_reduce(posk0, prod0, AX.X, ALU.add))
            wait(ve, c_sc, b - 1)
            ve.tensor_copy(idx_b[:, :, 0], posk0).then_inc(c_slot.sem, 1)
            ve.tensor_copy(slot[:, :, bass.ds(b, 1)], posk0.unsqueeze(2)).then_inc(c_slot.sem, 1)

        def scatter(b):
            pool_gate((c_slot, b, 5), (c_xs, b, None))
            for n in range(TOP):
                ge.indirect_dma_start(slots_x, bass.IndirectOffsetOnAxis(ap=idx_b[:, n, :], axis=0),
                                      xs0, None).then_inc(c_sc.sem, 16)

        def transpose_router(b):
            wait(te, nr.c_xh, b)
            transpose_blocks(xr, CB, S).then_inc(rt.sem, 1)
        J = lambda f, c: (lambda b: f(b, c))
        jobs0 = [(0, 0, J(x0.queries, 1), "vector", J(x0.spread_queries, 1), x0.q, 2),
                 (1, 0, J(x0.keys, 1), "scalar", J(x0.copy_keys, 1), x0.kt, 2),
                 (4, 1, transpose_rows0, "scalar", copy_rows0, x0.xtv, 1),
                 (5, -2, rank, "vector", assign_slots, c_slot, 2),
                 (6, 0, J(x0.values, 1), "vector", J(x0.copy_values, 1), x0.v, 2),
                 (7, -1, x0.transpose_o, "scalar", x0.copy_o, x0.otv, 1),
                 (8, -1, project_o0, "vector", add_residual0, res0, 1),
                 (9, 1, J(x0.queries, 0), "vector", J(x0.spread_queries, 0), x0.q, 1),
                 (11, 1, J(x0.keys, 0), "scalar", J(x0.copy_keys, 0), x0.kt, 1),
                 (12, -1, transpose_router, "scalar", copy_router, rtv, 1),
                 (14, 1, J(x0.values, 0), "vector", J(x0.copy_values, 0), x0.v, 1),
                 (15, -1, logits0, "vector", copy_logits0, rlv, 1)]
        rowsX = lambda b: X[:, b, :]
        x_loaded = lambda b: once(b, [(s_x, 0, None)]) + once(b - 1, [(s_x1, 0, None)])
        extra0 = [(0, "vector", 1, lambda b: n0.bn_stats(b, rowsX(b), x_loaded(b))),
                  (0, "vector", 1, lambda b: n0.bn_aggr(b)), (0, "gpsimd", 1, lambda b: n0.power(b)),
                  (2, "vector", 1, lambda b: n0.apply(b, rowsX(b), x0.xh, [(x0.xt, b - 1, None)])),
                  (8, "vector", -1, lambda b: nr.bn_stats(b, rowsX(b), [(res0, b, None)])),
                  (8, "vector", -1, lambda b: nr.bn_aggr(b)), (8, "gpsimd", -1, lambda b: nr.power(b)),
                  (10, "vector", -1, lambda b: nr.apply(b, rowsX(b), xr, [(rt, b - 1, None), (c_xs, b - 1, None)])),
                  (1, "vector", -2, lambda b: pick(b, 0)), (3, "vector", -2, lambda b: pick(b, 1)),
                  (5, "gpsimd", -2, scatter), (10, "gpsimd", -1, keep_rows)]
        def load_experts(b):
            se.dma_start(w1e.rearrange("p e n m -> p (e n) m")[:, b, :],
                         t["w1e"].rearrange("e (n p) m -> (e n) p m", p=P)[b, :, :]).then_inc(s_we.sem, 16)
            se.dma_start(w2e.rearrange("p e (a n) m -> p (e a) n m", n=2)[:, b, :, :],
                         t["w2e"].rearrange("e (a n p) m -> (e a) p n m", p=P, n=2)[b, :, :, :]).then_inc(s_we.sem, 16)
        def load_x(b):
            if isinstance(b, int) and b == 0:
                se.dma_start(X[:, 1:B, :], t["x"][1:B, :, :].rearrange("b s c -> s b c")).then_inc(s_x1.sem, 16)
        a0.add("sync", 1, load_ctxT)
        a0.add("sync", 1, load_x)
        a0.add("sync", 0, load_experts)
        a0.add("tensor", 1, lambda b: once(b, [0]) and wait(te, s_w0, 0))
        x0.plan(a0, jobs0, extra0)

        class Chain:

            def __init__(self, tag, eng):
                self.c, self.n, self.eng = Counter(nc, tag), 0, eng

            def __call__(self, ins):
                ins.then_inc(self.c.sem, 1)
                self.n += 1
                return self.n

            def settle(self):
                self.eng.wait_ge(self.c.sem, self.n)

        over_e = lambda a: a.unsqueeze(2).broadcast_to([S, B, E])
        (eq, cand, oh1, oh2, lg2, prod, cm, m1, m2) = carve(work, *[(S, B, E)] * 6, *[(S, B)] * 3)
        cnt, over, nt, ntc, past, past_nt, eidf, done_, row = carve(
            wa1[:, 2048:3072], (S, E), (S, E, B * S // P), (S, E), (S, E), (1, 40, E), (1, 40, E), (1, 40), (1, 40), (1, 40))
        start, gap, jump, in_, in_gap, off = carve(
            work[:, 9472:10260], (S, E), (S, E), (S, E - 1), (S, TOP * B, E - 1), (S, TOP * B, E - 1), (S, TOP * B))
        eid, rowid, tail = sb("eid", [1, 40], U32), sb("rowid", [1, 40], U32), sb("tail", [1, E], U32)
        c_ee, c_idx, c_tl, c_routed = (Counter(nc, x) for x in ("ee", "idx", "tail", "routed"))
        chain = Chain("route", ve)

        def top_two(step):
            iota8 = k["iota"][0:S, 0:E].unsqueeze(1).broadcast_to([S, B, E])
            src = LG[:, :, :]
            for m, oh in ((m1, oh1), (m2, oh2)):
                step(ve.tensor_reduce(m, src, AX.X, ALU.max))
                step(ve.tensor_tensor(eq, src, over_e(m), ALU.is_equal))
                step(ve.scalar_tensor_tensor(cand, eq, -100.0, iota8, ALU.mult, ALU.add))
                step(ve.tensor_reduce(cm, cand, AX.X, ALU.min))
                step(ve.tensor_tensor(oh, cand, over_e(cm), ALU.is_equal))
                if oh is oh1:
                    step(ve.scalar_tensor_tensor(lg2, oh1, -3.0e38, LG[:, :, :], ALU.mult, ALU.add))
                    src = lg2

        def route_vector():
            def step(ins):
                chain(ins)
                chain.settle()
            wait(ve, c_slot, B - 1)
            ve.tensor_copy(tail[:, :], next_slot[0:1, :]).then_inc(c_tl.sem, 1)
            step(ve.tensor_tensor(cnt, next_slot, k["region"][0:S, :], ALU.subtract))
            n = B * S // P
            step(ve.tensor_tensor(over, cnt.unsqueeze(2).broadcast_to([S, E, n]),
                                  k["steps"][0:S, :].unsqueeze(1).broadcast_to([S, E, n]), ALU.is_gt))
            step(ve.tensor_reduce(nt, over, AX.X, ALU.add))
            step(ve.tensor_tensor_scan(ntc, k["ones"][0:S, 0:E], nt, 0.0, ALU.mult, ALU.add))
            step(ve.tensor_tensor(past, k["iota"][0:1, :].unsqueeze(2).broadcast_to([1, 40, E]),
                                  ntc[0:1, :].unsqueeze(1).broadcast_to([1, 40, E]), ALU.is_ge))
            step(ve.tensor_reduce(eidf, past, AX.X, ALU.add))
            step(ve.tensor_tensor(past_nt, past, nt[0:1, :].unsqueeze(1).broadcast_to([1, 40, E]), ALU.mult))
            step(ve.tensor_reduce(done_, past_nt, AX.X, ALU.add))
            step(ve.tensor_tensor(row, k["iota"][0:1, :], done_, ALU.subtract))
            step(ve.tensor_scalar(row, row, float(P), None, ALU.mult))
            step(ve.scalar_tensor_tensor(row, eidf, float(ROOM), row, ALU.mult, ALU.add))
            step(ve.tensor_copy(rowid[:, :], row))
            step(ve.tensor_scalar(eidf, eidf, float(E - 1), None, ALU.min))
            step(ve.tensor_copy(eid[:, :], eidf))
            ve.tensor_copy(junk[:, word("vector")], eidf[:, 0:1]).then_inc(c_idx.sem, 1)
            flat = slot[:, :, :].rearrange("p k b -> p (k b)")
            step(ve.tensor_tensor(start, ntc, nt, ALU.subtract))
            step(ve.scalar_tensor_tensor(gap, start, -float(P), k["region"][0:S, :], ALU.mult, ALU.add))
            step(ve.tensor_tensor(jump, gap[:, 1:E], gap[:, 0:E - 1], ALU.subtract))
            step(ve.tensor_tensor(in_, flat.unsqueeze(2).broadcast_to([S, TOP * B, E - 1]),
                                  k["region"][0:S, 1:E].unsqueeze(1).broadcast_to([S, TOP * B, E - 1]), ALU.is_ge))
            step(ve.tensor_tensor(in_gap, in_, jump.unsqueeze(1).broadcast_to([S, TOP * B, E - 1]), ALU.mult))
            step(ve.tensor_reduce(off, in_gap, AX.X, ALU.add))
            step(ve.tensor_tensor(off, flat, off, ALU.subtract))
            step(ve.tensor_copy(idx_all[:, :, :].rearrange("p k b -> p (k b)"), off))
            ve.wait_ge(c_ee.sem, 1)
            step(ve.tensor_scalar(p12[:, 0, :], p12[:, 1, :], 1.0, None, ALU.add))
            step(ve.reciprocal(p12[:, 0, :], p12[:, 0, :]))
            ve.tensor_tensor(p12[:, 1, :], p12[:, 0, :], p12[:, 1, :], ALU.mult).then_inc(c_routed.sem, 1)

        def route_scalar():
            wait(ae, c_pick, B - 1)
            ae.activation(p12[:, 1, :], p12[:, 1, :], ACT.Exp).then_inc(c_ee.sem, 1)

        def zero_tails(eng, experts):
            wait(eng, c_tl, 0)
            for e in experts:
                at = eng.value_load(tail[0:1, e:e + 1], min_val=0, max_val=E * ROOM - P)
                eng.dma_start(slots_x[bass.ds(at, P), :], zeros[:, 0, :]).then_inc(c_tails.sem, 16)

        XA, XO, hT, hid, wq2, wk2, wv2, a2_li1, a2_li2, a2_li3, f1w, f2w = carve(
            arena, (S, B, C), (S, B, C), (P, CB, B * S), (P, FB, GS), (P, CB, 512), (P, 1, 512), (P, 1, 512),
            (P, 4, C), (P, CB, F1), (P, FB, C), (P, CB, F1), (P, FB, C))
        wq1, wk1, wv1, a1_li1, a1_li2, a1_li3 = carve(
            wa1, (P, CB, 512), (P, CB, 512), (P, CB, 512), (P, 4, C), (P, CB, F1), (P, FB, C))
        wg = sb("wg", [P, CB, E])
        s_wa1, s_rows, s_wa2 = Counter(nc, "wa1", 6, 16), Counter(nc, "rows", len(ROWS), 16), Counter(nc, "wa2", 9, 16)
        R = UNROLL
        xg, xgT, hb, hT_, yg = carve(work, (P, R, C), (P, R, CB, P), (P, R, F0), (P, R, F0 // P, P), (P, R, C))
        tiles = Pipeline(TILES // R)
        m_ld, m_st = ([Counter(nc, f"m_{x}{r}", 1, 16) for r in range(R)] for x in ("ld", "st"))
        (m_gt, m_gtv, m_h, m_hb, m_gl, m_ht, m_htv, m_y, m_yg) = (
            Counter(nc, "m_" + x) for x in ("gt", "gtv", "h", "hb", "gl", "ht", "htv", "y", "yg"))
        psGT, psH, psHT, psY = psM, psum, psum[:, 5, :], psO

        def expert(eng, j):
            return eng.value_load(eid[0:1, bass.ds(j, 1)], min_val=0, max_val=E - 1)

        def tile_row(j):
            return se.value_load(rowid[0:1, bass.ds(j, 1)], min_val=0, max_val=SLOTS - P)

        def m_load(j, r, it):
            at = tile_row(j)
            if isinstance(j, int) and j == 0:
                wait(se, c_sc, B - 1)
                wait(se, c_tails, 0)
                wait(se, c_fill, 0)
            wait(se, m_gt, j - R)
            se.dma_start(xg[:, r, :], slots_x[bass.ds(at, P), :]).then_inc(m_ld[r].sem, 16)

        def m_transpose(j, r, it):
            wait(te, m_ld[r], it)
            wait(te, m_gtv, j - 1)
            for cb in range(CB):
                ins = te.transpose(psGT[:, cb * P:(cb + 1) * P], xg[:, r, cb * P:(cb + 1) * P], ident)
            ins.then_inc(m_gt.sem, 1)

        def m_copy_x(j, r, it):
            wait(ae, m_gt, j)
            wait(ae, m_h, j - R)
            ae.activation(xgT[:, r, :, :], psGT[:, 0:C].rearrange("p (n w) -> p n w", n=CB), ACT.Copy).then_inc(m_gtv.sem, 1)

        def m_up(j, r, it):
            e = expert(te, j)
            if isinstance(j, int) and j == 0:
                wait(te, s_we, 0)
            wait(te, m_gtv, j)
            wait(te, m_hb, j - R)
            for cb in range(CB):
                ins = te.matmul(psH[:, r, :], xgT[:, r, cb, :], w1e[:, e, cb, :], start=cb == 0, stop=cb == CB - 1)
            ins.then_inc(m_h.sem, 1)

        def m_bias_up(j, r, it):
            e = expert(ve, j)
            wait(ve, m_h, j)
            wait(ve, m_ht, j - R)
            ve.tensor_tensor(hb[:, r, :], psH[:, r, :], b1e[:, e, :], ALU.add).then_inc(m_hb.sem, 1)

        def m_gelu(j, r, it):
            wait(ae, m_hb, j)
            ae.activation(hb[:, r, :], hb[:, r, :], ACT.Gelu).then_inc(m_gl.sem, 1)

        def m_transpose_h(j, r, it):
            wait(te, m_gl, j)
            wait(te, m_htv, j - 1)
            for fb in range(F0 // P):
                ins = te.transpose(psHT[:, fb * P:(fb + 1) * P], hb[:, r, fb * P:(fb + 1) * P], ident)
            ins.then_inc(m_ht.sem, 1)

        def m_copy_h(j, r, it):
            wait(ve, m_ht, j)
            wait(ve, m_y, j - R)
            ve.tensor_copy(hT_[:, r, :, :], psHT.rearrange("p (n w) -> p n w", n=F0 // P)).then_inc(m_htv.sem, 1)

        def m_down(j, r, it):
            e = expert(te, j)
            wait(te, m_htv, j)
            wait(te, m_yg, j - 1)
            n = F0 // P
            for fb in range(n):
                ins = te.matmul(psY[:, 0:C], hT_[:, r, fb, :], w2e[:, e, fb, :], start=fb == 0, stop=fb == n - 1)
            ins.then_inc(m_y.sem, 1)

        def m_bias_down(j, r, it):
            e = expert(ve, j)
            wait(ve, m_y, j)
            wait(ve, m_st[r], it - 1)
            ve.tensor_tensor(yg[:, r, :], psY[:, 0:C], b2e[:, e, :], ALU.add).then_inc(m_yg.sem, 1)

        def m_store(j, r, it):
            wait(se, m_yg, j)
            se.dma_start(slots_y[bass.ds(j * P, P), :], yg[:, r, :]).then_inc(m_st[r].sem, 16)

        def load_a1():
            dma = lambda dst, src, c_: se.dma_start(dst, src).then_inc(c_.sem, 16)
            wait(se, c_routed, 0)
            for n, name in enumerate(ROWS):
                dma(rows[name], t["rows"][n, :].partition_broadcast(S), s_rows)
            for n, dst in (("wk", wk1), ("wv", wv1)):
                dma(dst, t["a1_" + n].rearrange("(n p) m -> p n m", p=P), s_wa1)
        tiles.add("sync", 0, lambda it: once(it, [0]) and load_a1())
        for u in range(R):
            def put(who, f, lag):
                d, r = divmod(u - lag, R)
                tiles.add(who, d, lambda it, f=f, r=r: f(it * R + r, r, it))
            put("sync", m_load, -3)
            put("tensor", m_transpose, -1)
            put("scalar", m_copy_x, -1)
            put("tensor", m_up, 0)
            put("vector", m_bias_up, 0)
            put("scalar", m_gelu, 0)
            put("tensor", m_transpose_h, 1)
            put("vector", m_copy_h, 1)
            put("tensor", m_down, 2)
            put("vector", m_bias_down, 2)
            put("sync", m_store, 2)

        c_g, c_cmb, c_ib = Counter(nc, "gather", TOP, 16), Counter(nc, "combine", TOP), Counter(nc, "idx_b")
        (yk,) = carve(work[:, 8960:9472], (S, TOP, C))

        def gather(b):
            if isinstance(b, int) and b == 0:
                for r in range(R):
                    wait(ge, m_st[r], TILES // R - 1)
            pool_gate((c_cmb, b - 1, None))
            ge.tensor_copy(idx_b[:, :, :], idx_all[:, :, bass.ds(b, 1)]).then_inc(c_ib.sem, 1)
            pool_gate((c_ib, b, None))
            for n in range(TOP):
                ge.indirect_dma_start(yk[:, n, :], None, slots_y,
                                      bass.IndirectOffsetOnAxis(ap=idx_b[:, n, :], axis=0)).then_inc(c_g.sem, 16)

        def combine(b):
            for n in range(TOP):
                if n:
                    wait(ve, c_cmb, b, n)
                else:
                    wait(ve, c_g, b)
                ve.scalar_tensor_tensor(X[:, b, :], yk[:, n, :], p12[:, n, bass.ds(b, 1)], X[:, b, :],
                                        ALU.mult, ALU.add).then_inc(c_cmb.sem, 1)


        HB = 512 // P
        XH = lambda cb: slice(cb * P, (cb + 1) * P)

        class Residual:

            def __init__(self, tag, norm, xb, scaled, ln, pre):
                self.norm, self.xb, self.ln, self.pre = norm, xb, ln, pre
                self.xs = scaled
                self.xa, self.fin = Counter(nc, tag + "_xa", 3), Counter(nc, tag + "_fin", 3 if pre == "a2" else 2)

            def affine(self, b):
                for counter, item, k_ in once(b, [(s_rows, 0, None)]):
                    wait(ge, counter, item, k_)
                wait(ge, self.norm.c_xh, b)
                ge.tensor_tensor(self.xs, self.xb, rows[self.ln + "_g"], ALU.mult).then_inc(self.xa.sem, 1)
                pool_gate((self.xa, b, 1))
                ge.tensor_tensor(XA[:, b, :], self.xs, rows[self.ln + "_b"], ALU.add).then_inc(self.xa.sem, 1)
                pool_gate((self.xa, b, 2))
                ge.tensor_tensor(XO[:, b, :], XA[:, b, :], rows[self.pre + "_li1_b"], ALU.add).then_inc(self.xa.sem, 1)

            def finish(self, b, norm3):
                pool_gate((norm3.c_xh, b, None))
                ge.tensor_tensor(XO[:, b, :], XO[:, b, :], XA[:, b, :], ALU.add).then_inc(self.fin.sem, 1)
                pool_gate((self.fin, b, 1))
                ge.tensor_tensor(XO[:, b, :], XO[:, b, :], rows[self.pre + "_li3_b"], ALU.add).then_inc(self.fin.sem, 1)
                if self.pre == "a2":
                    pool_gate((self.fin, b, 2))
                    ge.tensor_tensor(XO[:, b, :], XO[:, b, :], X[:, b, :], ALU.add).then_inc(self.fin.sem, 1)

        def affine_copy(dst, src, g, b_, cb):
            return ae.activation(dst, src, ACT.Identity, bias=b_[:, cb:cb + 1], scale=g[:, cb:cb + 1])

        a1 = Pipeline(B)
        Qb, KT1, V1, Pr1, PT1, xh1, xTq, xTy, On1, OT1, y0, xb1, xh3, xs1 = carve(
            work[:, 0:8960], (P, 4, 4, S), (P, 4, S), (S, 512), (S, 2, 4 * S), (S, 2, 4 * S), (S, C), (P, CB, S),
            (P, CB, S), (S, 512), (P, 4, S), (S, C), (S, C), (S, C), (S, C))
        nA, nB, nC, nD = Norm("nA", follows=n0), Norm("nB", follows=nr), Norm("nC"), Norm("nD")
        r1 = Residual("r1", nB, xb1, xs1, "ln1", "a1")
        c = lambda name, per=1, step=1: Counter(nc, "a1_" + name, per, step)
        u_xt, u_xtv, u_qk, u_q, u_k, u_vp, u_v = c("xt"), c("xtv"), c("qk", 4), c("q", 4), c("k", 4), c("vp"), c("v")
        u_s, u_mx, u_e, u_tr, u_pt, u_pv = (c(x, 4) for x in ("s", "mx", "e", "tr", "pt", "pv"))
        u_rcp, u_on, u_ot, u_otv, u_li, u_xo, u_ht, u_htv = (c(x) for x in ("rcp", "on", "ot", "otv", "li", "xo", "ht", "htv"))

        def u_scores(b, g):
            wait(te, u_q, b, g + 1)
            wait(te, u_k, b, g + 1)
            wait(te, u_e, b, g + 1 - 2)
            for i in range(4):
                ins = te.matmul(psS[0:S, g % 2, i * S:(i + 1) * S], Qb[:, g, i, :], KT1[:, g, :], start=True, stop=True)
            ins.then_inc(u_s.sem, 1)

        def u_max(b, g):
            wait(ve, u_s, b, g + 1)
            ve.tensor_reduce(nmax[:, 4 * g:4 * g + 4], psS[0:S, g % 2, 0:4 * S].rearrange("p (h s) -> p h s", h=4),
                             AX.X, ALU.max, negate=True).then_inc(u_mx.sem, 1)

        def u_exp(b, g):
            wait(ae, u_mx, b, g + 1)
            wait(ae, u_tr, b, g + 1 - 2)
            for i in range(4):
                h = 4 * g + i
                ins = ae.activation(Pr1[:, g % 2, i * S:(i + 1) * S], psS[0:S, g % 2, i * S:(i + 1) * S], ACT.Exp,
                                    bias=nmax[:, h:h + 1], accum_out=sums[:, bass.ds(b * H + h, 1)])
            ins.then_inc(u_e.sem, 1)

        def u_transpose(b, g):
            wait(te, u_e, b, g + 1)
            wait(te, u_pt, b, g + 1 - 2)
            for i in range(4):
                ins = te.transpose(psT[0:S, g % 2, i * S:(i + 1) * S], Pr1[:, g % 2, i * S:(i + 1) * S], ident[0:S, 0:S])
            ins.then_inc(u_tr.sem, 1)

        def u_mask(b, g):
            wait(ve, u_tr, b, g + 1)
            wait(ve, u_pv, b, g + 1 - 2)
            ve.tensor_tensor(PT1[:, g % 2, :].rearrange("p (h s) -> p h s", h=4),
                             psT[0:S, g % 2, 0:4 * S].rearrange("p (h s) -> p h s", h=4),
                             k["after"][0:S, :].unsqueeze(1).broadcast_to([S, 4, S]), ALU.mult).then_inc(u_pt.sem, 1)

        def u_values(b, g):
            wait(te, u_pt, b, g + 1)
            if g == 0:
                wait(te, u_v, b)
                wait(te, u_on, b - 1)
            for i in range(4):
                h = 4 * g + i
                ins = te.matmul(psO[0:S, h * 32:(h + 1) * 32], PT1[:, g % 2, i * S:(i + 1) * S],
                                V1[:, h * 32:(h + 1) * 32], start=True, stop=True)
            ins.then_inc(u_pv.sem, 1)

        def u_recip(b):
            wait(ve, u_e, b)
            wait(ve, u_on, b - 1)
            ve.reciprocal(rsum[:, :], sums[:, bass.ds(b * H, H)]).then_inc(u_rcp.sem, 1)

        def u_divide(b):
            wait(ve, u_rcp, b)
            wait(ve, u_pv, b)
            wait(ve, u_ot, b - 1)
            ve.tensor_tensor(On1.rearrange("p (h d) -> p h d", h=H), psO[0:S, :].rearrange("p (h d) -> p h d", h=H),
                             rsum[:, :].unsqueeze(2).broadcast_to([S, H, 32]), ALU.mult).then_inc(u_on.sem, 1)

        def u_vproj(b, bank):
            for cb in range(CB):
                ins = te.matmul(bank[0:S, :], xTy[:, cb, :], wv1[:, cb, :], start=cb == 0, stop=cb == CB - 1)
            ins.then_inc(u_vp.sem, 1)

        def u_vcopy(b, bank):
            wait(ae, u_vp, b)
            wait(ae, u_pv, b - 1)
            ae.activation(V1, bank[0:S, :], ACT.Copy).then_inc(u_v.sem, 1)

        def u_xtr(b, bank):
            wait(te, nC.c_xh, b)
            transpose_blocks(xh1, CB, S, bank).then_inc(u_xt.sem, 1)

        def u_xcopy(b, bank):
            wait(ae, u_xt, b)
            for cb in range(CB):
                affine_copy(xTq[:, cb, :], bank[:, cb * S:(cb + 1) * S], k["a1_lnx_g"], k["a1_lnx_b"], cb)
                ins = affine_copy(xTy[:, cb, :], bank[:, cb * S:(cb + 1) * S], k["a1_lny_g"], k["a1_lny_b"], cb)
            ins.then_inc(u_xtv.sem, 1)

        def u_qkproj(b, bank, g):
            wait(te, u_xtv, b)
            for at_, w, x in ((0, wq1, xTq), (S, wk1, xTy)):
                for cb in range(CB):
                    ins = te.matmul(bank[:, at_:at_ + S], w[:, cb, XH(g)], x[:, cb, :], start=cb == 0, stop=cb == CB - 1)
            ins.then_inc(u_qk.sem, 1)

        def u_qcopy(b, bank, g):
            wait(ve, u_qk, b, g + 1)
            wait(ve, u_k, b, g + 1)
            wait(ve, u_s, b - 1, g + 1)
            ve.tensor_tensor(Qb[:, g, :, :], bank[:, 0:S].unsqueeze(1).broadcast_to([P, 4, S]),
                             k["mask1"].unsqueeze(2).broadcast_to([P, 4, S]), ALU.mult).then_inc(u_q.sem, 1)

        def u_kcopy(b, bank, g):
            wait(ae, u_qk, b, g + 1)
            wait(ae, u_s, b - 1, g + 1)
            ae.activation(KT1[:, g, :], bank[:, S:2 * S], ACT.Copy).then_inc(u_k.sem, 1)

        def u_otr(b, bank):
            wait(te, u_on, b)
            transpose_blocks(On1, HB, S, bank).then_inc(u_ot.sem, 1)

        def u_ocopy(b, bank):
            wait(ae, u_ot, b)
            ae.activation(OT1, psum_rows(HB, S, bank), ACT.Copy).then_inc(u_otv.sem, 1)

        def project_out(OT_, w, copied, counter):
            def action(b, bank=psM):
                wait(te, copied, b)
                for cb in range(HB):
                    ins = te.matmul(bank[0:S, 0:C], OT_[:, cb, :], w[:, cb, :], start=cb == 0, stop=cb == HB - 1)
                ins.then_inc(counter.sem, 1)
            return action

        def add_out(li, res, counter):
            def action(b, bank=psM):
                wait(ve, li, b)
                wait(ve, res.xa, b)
                ve.tensor_tensor(XO[:, b, :], bank[0:S, 0:C], XO[:, b, :], ALU.add).then_inc(counter.sem, 1)
            return action

        def transpose_h(norm, xh_, counter):
            def action(b, bank=psM):
                wait(te, norm.c_xh, b)
                transpose_blocks(xh_, CB, S, bank).then_inc(counter.sem, 1)
            return action

        def copy_h(done, tag, counter):
            def action(b, bank=psM):
                wait(ae, done, b)
                for cb in range(CB):
                    ins = affine_copy(hT[:, cb, bass.ds(b * S, S)], bank[:, cb * S:(cb + 1) * S],
                                      k[tag + "_ln3_g"], k[tag + "_ln3_b"], cb)
                ins.then_inc(counter.sem, 1)
            return action

        G = lambda f, g: (lambda b: f(b, g))
        GJ = lambda f, g: (lambda b, bank: f(b, bank, g))
        QK = lambda g, at_, d: (at_, d, GJ(u_qkproj, g), [("scalar", GJ(u_kcopy, g)), ("vector", GJ(u_qcopy, g))], u_q, g + 1)
        jobs1 = [QK(2, "0B", 0),
                 QK(3, "0C", 0),
                 ("1A", -2, transpose_h(nD, xh3, u_ht), [("scalar", copy_h(u_ht, "a1", u_htv))], u_htv, 1),
                 ("1C", 0, u_vproj, [("scalar", u_vcopy)], u_v, 1),
                 ("2A", 1, u_xtr, [("scalar", u_xcopy)], u_xtv, 1),
                 ("2C", -1, u_otr, [("scalar", u_ocopy)], u_otv, 1),
                 QK(0, "3A", 1),
                 ("3B", -1, project_out(OT1, a1_li1, u_otv, u_li), [("vector", add_out(u_li, r1, u_xo))], u_xo, 1),
                 QK(1, "3C", 1)]
        job_banks = [psum[:, 2, :], psum[:, 3, :], psum[:, 6, :]]
        NB = len(job_banks)
        turns1 = [Turns(B, [(d, counter, ev) for _, d, _, _, counter, ev in jobs1[n::NB]]) for n in range(NB)]
        rowsXA, rowsXO = (lambda b: XA[:, b, :]), (lambda b: XO[:, b, :])
        for g in range(4):
            at = lambda lag: (0 if g >= lag else -1, (g - lag) % 4)
            a1.add("vector", 0, G(u_max, g))
            a1.add("tensor", 0, G(u_scores, g))
            if g == 0:
                a1.add("vector", 2, combine)
            d_, g_ = at(1)
            a1.add("vector", d_, G(u_mask, g_))
            for place in "ABC":
                if place == "B":
                    a1.add("scalar", 0, G(u_exp, g))
                    a1.add("tensor", d_, G(u_transpose, g_))
                if place == "C":
                    d, g2 = at(2)
                    a1.add("tensor", d, G(u_values, g2))
                for n, (where_, d, pe, copies, _, _) in enumerate(jobs1):
                    if where_ == f"{g}{place}":
                        def job1(b, n=n, pe=pe):
                            turns1[n % NB].wait_before(te, n // NB, b)
                            pe(b, job_banks[n % NB])
                        a1.add("tensor", d, job1)
                        for who, copy in copies:
                            a1.add(who, d, lambda b, n=n, copy=copy: copy(b, job_banks[n % NB]))
            if g == 0:
                nC.plan_apply(a1, 1, rowsXA, lambda b: xh1, lambda b: [(u_xt, b - 1, None)])
                nA.plan(a1, 2, rowsX, lambda b: [(c_cmb, b, None)])
            if g == 1:
                a1.add("vector", -1, u_recip)
                a1.add("vector", -1, u_divide)
                a1.add("gpsimd", 3, gather)
                nA.plan_apply(a1, 2, rowsX, lambda b: y0, lambda b: [(nB.c_xh, b - 1, None)])
                nB.plan(a1, 2, lambda b: y0, lambda b: [(nA.c_xh, b, None)])
            if g == 2:
                nB.plan_apply(a1, 2, lambda b: y0, lambda b: xb1, lambda b: [(r1.xa, b - 1, 1)])
                a1.add("gpsimd", 2, lambda b: r1.affine(b))
            if g == 3:
                nD.plan(a1, -1, rowsXO, lambda b: [(u_xo, b, None)])
                nC.plan(a1, 2, rowsXA, lambda b: [(r1.xa, b, 2)])
                nD.plan_apply(a1, -1, rowsXO, lambda b: xh3, lambda b: [(u_ht, b - 1, None)])
                a1.add("gpsimd", -1, lambda b: r1.finish(b, nD))

        class FeedForward:
            def __init__(self, tag, w1, bias, w2, func, ready, add, follows=None):
                self.w1, self.bias, self.w2, self.func, self.ready, self.post = w1, bias, w2, func, ready, add
                self.pipe = Pipeline(B // GB)
                old = follows.counters if follows else [None] * 4
                self.counters = [Counter(nc, f"{tag}_{name}", per, 1, items, o) for (name, per, items), o in zip(
                    (("h", FB, B // GB), ("gl", FB, B // GB), ("y", GB, B // GB), ("done", 1, B)), old)]
                self.h, self.gl, self.y, self.done = self.counters

            def up(self, g, f):
                if f == 0:
                    wait(te, self.ready, g * GB + GB - 1)
                wait(te, self.gl, g, f + 1 - 4)
                for cb in range(CB):
                    ins = te.matmul(psS[:, f % 4, 0:GS], self.w1[:, cb, XH(f)], hT[:, cb, bass.ds(g * GS, GS)],
                                    start=cb == 0, stop=cb == CB - 1)
                ins.then_inc(self.h.sem, 1)

            def act(self, g, f):
                wait(ae, self.h, g, f + 1)
                if f == 0:
                    wait(ae, self.y, g - 1)
                if self.bias is None:
                    ins = ae.activation(hid[:, f, :], psS[:, f % 4, 0:GS], self.func)
                else:
                    ins = ae.activation(hid[:, f, :], psS[:, f % 4, 0:GS], self.func, bias=self.bias[:, f:f + 1])
                ins.then_inc(self.gl.sem, 1)

            def down(self, g, q):
                if q == 0:
                    wait(te, self.gl, g)
                wait(te, self.done, g * GB + q - 2)
                for f in range(FB):
                    ins = te.matmul(psT[0:S, q % 2, 0:C], hid[:, f, q * S:(q + 1) * S], self.w2[:, f, :],
                                    start=f == 0, stop=f == FB - 1)
                ins.then_inc(self.y.sem, 1)

            def add(self, g, q):
                wait(ve, self.y, g, q + 1)
                self.post(g * GB + q, psT[0:S, q % 2, 0:C]).then_inc(self.done.sem, 1)

            def plan(self, each=()):
                def extras(slot):
                    for slot_, who, d, action in each:
                        if slot_ == slot:
                            self.pipe.add(who, d, action)
                for f in range(2, FB + 2):
                    extras(f - 2)
                    d, f = (0, f) if f < FB else (1, f - FB)
                    self.pipe.add("tensor", d, lambda g, f=f: self.up(g, f))
                    if d == 0:
                        self.pipe.add("scalar", 0, lambda g, f=f: self.act(g, f))
                for q in range(GB):
                    self.pipe.add("tensor", 0, lambda g, q=q: self.down(g, q))
                    self.pipe.add("vector", 0, lambda g, q=q: self.add(g, q))
                    extras(FB + q)
                for f in range(2):
                    self.pipe.add("scalar", 1, lambda g, f=f: self.act(g, f))

        def add_f1(b, y):
            wait(ve, r1.fin, b)
            return ve.tensor_tensor(XO[:, b, :], y, XO[:, b, :], ALU.add)
        f_1 = FeedForward("f1", a1_li2, k["a1_li2_b"], a1_li3, ACT.Gelu, u_htv, add_f1)
        a2 = Pipeline(B)
        x2 = Cross("a2", 32, wq2, wk2, wv2, k["mask1"], ctx_step=1, follows=x0)
        nE, nF, nG = (Norm(n, follows=old) for n, old in (("nE", nA), ("nF", nB), ("nG", nC)))
        nX = Norm("nX", LK, NK, follows=nD)
        xb2, xh4, xs2 = carve(wa1, (S, C), (S, C), (S, C))
        r2 = Residual("r2", nE, xb2, xs2, "ln2", "a2")
        s_cx = Counter(nc, "cx", 1, 16)
        v_li, v_xo, v_ht, v_htv, v_ct = (Counter(nc, "a2_" + n, follows=old) for n, old in (
            ("li", u_li), ("xo", u_xo), ("ht", u_ht), ("htv", u_htv), ("ct", u_xt)))

        def load_ctx(b):
            if isinstance(b, int) and b == 0:
                wait(se, f_1.y, 0, 1)
            wait(se, nX.c_xh, b - 1)
            se.dma_start(x2.cx, t["ctx"][b, :, :].rearrange("(n p) d -> p n d", p=LK)).then_inc(s_cx.sem, 16)

        def transpose_rows2(b):
            wait(te, nF.c_xh, b)
            transpose_blocks(x2.xh, CB, S).then_inc(x2.xt.sem, 1)

        def copy_rows2(b):
            wait(ae, x2.xt, b)
            for cb in range(CB):
                ins = affine_copy(x2.xT[:, cb, :], psM[:, cb * S:(cb + 1) * S], k["a2_lnx_g"], k["a2_lnx_b"], cb)
            ins.then_inc(x2.xtv.sem, 1)

        def transpose_ctx(b):
            wait(te, nX.c_xh, b)
            for kb in range(NK):
                ins = te.transpose(psM[:, kb * LK:(kb + 1) * LK], x2.cxh[:, kb, :], ident[0:LK, 0:LK])
            ins.then_inc(v_ct.sem, 1)

        def copy_ctx(b):
            wait(ae, v_ct, b)
            affine_copy(x2.ctxT, psM[:, 0:L], k["a2_lny_g"], k["a2_lny_b"], 0).then_inc(x2.ctx.sem, 1)

        Qj = lambda g, s_, d: (s_, d, J(x2.queries, g), "vector", J(x2.spread_queries, g), x2.q, g + 1)
        Kj = lambda g, s_, d: (s_, d, J(x2.keys, g), "scalar", J(x2.copy_keys, g), x2.kt, g + 1)
        Vj = lambda g, s_, d: (s_, d, J(x2.values, g), "vector", J(x2.copy_values, g), x2.v, g + 1)
        jobs2 = [Qj(2, 0, 0), Kj(2, 1, 0), Vj(2, 2, 0), Qj(3, 3, 0), Kj(3, 4, 0),
                 (5, 1, transpose_rows2, "scalar", copy_rows2, x2.xtv, 1),
                 Vj(3, 6, 0),
                 (7, 1, transpose_ctx, "scalar", copy_ctx, x2.ctx, 1),
                 (8, -1, x2.transpose_o, "scalar", x2.copy_o, x2.otv, 1),
                 (9, -1, project_out(x2.OT, a2_li1, x2.otv, v_li), "vector", add_out(v_li, r2, v_xo), v_xo, 1),
                 Kj(0, 10, 1), Vj(0, 11, 1), Qj(0, 12, 1), Qj(1, 13, 1),
                 (13, -1, transpose_h(nG, xh4, v_ht), "scalar", copy_h(v_ht, "a2", v_htv), v_htv, 1),
                 Kj(1, 14, 1), Vj(1, 15, 1)]
        norms2 = [(0, 0, "vector", lambda b: nE.bn_stats(b, XO[:, b, :], [(f_1.done, b, None)] if isinstance(b, int) else [])),
                  (0, 0, "vector", nE.bn_aggr), (0, 0, "gpsimd", nE.power),
                  (1, 1, "vector", lambda b: nX.bn_stats(b, x2.cx, [(s_cx, b, None)])),
                  (1, 1, "vector", nX.bn_aggr), (1, 1, "gpsimd", nX.power),
                  (1, 2, "vector", lambda b: nE.apply(b, XO[:, b, :], xb2, [(r2.xa, b - 1, 1)])),
                  (1, 2, "gpsimd", lambda b: r2.affine(b)),
                  (3, 4, "vector", lambda b: nF.bn_stats(b, XA[:, b, :], [(r2.xa, b, 2)])),
                  (3, 4, "vector", nF.bn_aggr), (3, 4, "gpsimd", nF.power),
                  (4, 6, "vector", lambda b: nF.apply(b, XA[:, b, :], x2.xh, [(x2.xt, b - 1, None)])),
                  (5, 7, "vector", lambda b: nX.apply(b, x2.cx, x2.cxh, [(v_ct, b - 1, None)]))]
        unless_first = lambda action: (lambda b: None if isinstance(b, int) and b == 0 else action(b))
        f_1.pipe.peel = 1
        f_1.plan([(slot_, who, 0, lambda g, action=action: action(0) if isinstance(g, int) and g == B // GB - 1 else None)
                  for _, slot_, who, action in norms2])
        extra2 = [(step, who, 1, unless_first(action)) for step, _, who, action in norms2]
        extra2 += [(9, "vector", -1, lambda b: nG.bn_stats(b, XO[:, b, :], [(v_xo, b, None)])),
                   (9, "vector", -1, nG.bn_aggr), (9, "gpsimd", -1, nG.power),
                   (11, "vector", -1, lambda b: nG.apply(b, XO[:, b, :], xh4, [(v_ht, b - 1, None)])),
                   (11, "gpsimd", -1, lambda b: r2.finish(b, nG))]
        a2.add("sync", 1, load_ctx)
        a2.add("tensor", 1, lambda b: once(b, [0]) and wait(te, s_wa2, 0))
        x2.plan(a2, jobs2, extra2)

        def add_f2(b, y):
            wait(ve, r2.fin, b)
            return ve.tensor_tensor(X[:, b, :], y, XO[:, b, :], ALU.add)
        f_2 = FeedForward("f2", a2_li2, k["a2_li2_b"], a2_li3, ACT.Gelu, v_htv, add_f2, f_1)
        nH = Norm("nH", follows=nE)
        g_t, g_tv, g_ta, g_l, g_lv = (Counter(nc, "g_" + n, follows=old) for n, old in (
            ("t", rt), ("tv", rtv), ("ta", u_rcp), ("l", rl), ("lv", rlv)))

        def transpose_g(b):
            wait(te, nH.c_xh, b)
            wait(te, g_tv, b - 1)
            transpose_blocks(xr, CB, S).then_inc(g_t.sem, 1)

        def copy_g_static(b):
            wait(ve, g_t, b)
            wait(ve, g_ta, b)
            wait(ve, g_l, b - 1)
            ve.tensor_copy(xTr, psum_rows(CB, S)).then_inc(g_tv.sem, 1)

        def copy_g(b):
            wait(ae, g_t, b)
            ae.activation(hT[:, :, bass.ds(b * S, S)], psum_rows(CB, S), ACT.Copy).then_inc(g_ta.sem, 1)

        def logits_g(b):
            wait(te, g_tv, b)
            wait(te, g_lv, b - 1)
            for cb in range(CB):
                ins = te.matmul(psO[0:S, 0:E], xTr[:, cb, :], wg[:, cb, :], start=cb == 0, stop=cb == CB - 1)
            ins.then_inc(g_l.sem, 1)

        def copy_logits_g(b):
            wait(ve, g_l, b)
            ve.tensor_copy(LG[:, b, :], psO[0:S, 0:E]).then_inc(g_lv.sem, 1)
        of = lambda q, f: (lambda g: f(g * GB + q))
        router = [part for q in range(GB) for part in (
            (2 * q, "vector", -1, of(q, lambda b: nH.bn_stats(b, X[:, b, :], [(f_2.done, b, None)]))),
            (2 * q, "vector", -1, of(q, nH.bn_aggr)), (2 * q, "gpsimd", -1, of(q, nH.power)),
            (2 * q + 1, "vector", -1, of(q, lambda b: nH.apply(b, X[:, b, :], xr, [(g_t, b - 1, None)]))),
            (2 * q + 2, "tensor", -1, of(q, transpose_g)), (2 * q + 2, "scalar", -1, of(q, copy_g)),
            (2 * q + 3, "vector", -1, of(q, copy_g_static)),
            (2 * q + 4, "tensor", -1, of(q, logits_g)), (2 * q + 5, "vector", -1, of(q, copy_logits_g)))]
        f_2.plan(router)

        gate_w = sb("gate_w", [S, B])
        c_gd, c_ge = Counter(nc, "gd"), Counter(nc, "ge")
        gchain = Chain("gating", ve)
        g_e, = carve(work[:, 8000:9000], (S, B, E))
        g_den, g_1, g_2 = carve(work[:, 9000:10000], *[(S, B)] * 3)

        def gating_vector():
            def step(ins):
                gchain(ins)
                gchain.settle()
            wait(ve, g_lv, B - 1)
            top_two(step)
            ve.tensor_tensor(g_e, LG[:, :, :], over_e(m1), ALU.subtract).then_inc(c_gd.sem, 1)
            ve.wait_ge(c_ge.sem, 1)
            step(ve.tensor_reduce(g_den, g_e, AX.X, ALU.add))
            step(ve.reciprocal(g_den, g_den))
            step(ve.tensor_tensor(g_e, g_e, over_e(g_den), ALU.mult))
            for oh, dst in ((oh1, g_1), (oh2, g_2)):
                step(ve.tensor_tensor(prod, oh, g_e, ALU.mult))
                step(ve.tensor_reduce(dst, prod, AX.X, ALU.add))
            step(ve.tensor_tensor(g_den, g_1, g_2, ALU.add))
            step(ve.tensor_scalar(g_den, g_den, float(np.finfo(np.float32).eps), None, ALU.max))
            step(ve.reciprocal(g_den, g_den))
            step(ve.tensor_tensor(g_1, g_1, g_den, ALU.mult))
            step(ve.tensor_tensor(g_2, g_2, g_den, ALU.mult))
            step(ve.tensor_tensor(gate_w[:, :], g_1, g_2, ALU.add))

        def gating_scalar():
            ae.wait_ge(c_gd.sem, 1)
            ae.activation(g_e, g_e, ACT.Exp).then_inc(c_ge.sem, 1)

        def add_f3(b, y):
            return ve.scalar_tensor_tensor(X[:, b, :], y, gate_w[:, bass.ds(b, 1)], X[:, b, :], ALU.mult, ALU.add)
        f_3 = FeedForward("f3", f1w, None, f2w, ACT.Relu, g_ta, add_f3, f_2)

        def store(b):
            wait(se, f_3.done, b)
            se.dma_start(out[b, :, :], X[:, b, :]).then_inc(s_out.sem, 16)
        f_3.plan([(FB + q, "sync", 0, of(q, store)) for q in range(GB)]
                 + [(4, "scalar", 0, lambda g: once(g, [0]) and gating_scalar())])

        def layer1_sync(eng, dma, blocks):
            wait(eng, c_cmb, B - 1)
            for n, dst in (("a2_wq", wq2), ("a2_wk", wk2), ("a2_wv", wv2), ("a2_li1", a2_li1), ("a2_li2", a2_li2),
                           ("a2_li3", a2_li3), ("f1", f1w), ("f2", f2w), ("wg", wg[:, :, :])):
                dma(dst, blocks(t[n]), s_wa2)
            a2.run("sync", eng)
            f_3.pipe.run("sync", eng)
            wait(eng, s_out, 0)

        def layer1(name, eng):
            if name == "tensor":
                wait(eng, s_wa1, 0)
            a1.run(name, eng)
            f_1.pipe.run(name, eng)
            a2.run(name, eng)
            f_2.pipe.run(name, eng)
            if name == "vector":
                gating_vector()
            f_3.pipe.run(name, eng)
        with nc.Block() as block:
            @block.sync
            def _(eng):
                dma = lambda dst, src, c_: eng.dma_start(dst, src).then_inc(c_.sem, 16)
                blocks = lambda w: w.rearrange("(n p) m -> p n m", p=P)
                dma(X[:, 0:1, :], t["x"][0:1, :, :].rearrange("b s c -> s b c"), s_x)
                dma(const[:, :], t["const"], s_const)
                dma(cols[:, :], t["cols"], s_const)
                dma(wq0, blocks(t["wq0"]), s_w0)
                dma(wk0[:, 0, :], t["wkv0"][:, 0:C], s_w0)
                dma(wv0[:, 0, :], t["wkv0"][:, C:2 * C], s_w0)
                dma(wo0, blocks(t["wo0"]), s_w0)
                dma(rw[:, :, :], blocks(t["rw"]), s_w0)
                a0.run("sync", eng)
                dma(b1e, t["b1e"].partition_broadcast(P), s_we)
                dma(b2e, t["b2e"].partition_broadcast(P), s_we)
                wait(eng, c_zero, 0)
                dma(slots_x[E * ROOM:SLOTS, :].rearrange("(p r) c -> p r c", p=P), zeros, c_fill)
                for n, dst in (("wq", wq1), ("li1", a1_li1), ("li2", a1_li2), ("li3", a1_li3)):
                    dma(dst, blocks(t["a1_" + n]), s_wa1)
                zero_tails(eng, range(0, E, 2))
                wait(eng, c_sc, B - 1)
                wait(eng, c_idx, 0)
                tiles.run("sync", eng)
                layer1_sync(eng, dma, blocks)

            @block.tensor
            def _(eng):
                wait(eng, s_const, 0)
                a0.run("tensor", eng)
                eng.wait_ge(c_idx.sem, 1)
                tiles.run("tensor", eng)
                layer1("tensor", eng)

            @block.scalar
            def _(eng):
                wait(eng, s_const, 0)
                a0.run("scalar", eng)
                zero_tails(eng, range(1, E, 2))
                route_scalar()
                tiles.run("scalar", eng)
                layer1("scalar", eng)

            @block.vector
            def _(eng):
                ve.memset(zeros, 0.0).then_inc(c_zero.sem, 1)
                wait(eng, s_const, 0)
                ve.tensor_copy(next_slot, k["region"][0:S, :]).then_inc(c_zero.sem, 1)
                ve.wait_ge(c_zero.sem, 2)
                a0.run("vector", eng)
                route_vector()
                tiles.run("vector", eng)
                layer1("vector", eng)

            @block.gpsimd
            def _(eng):
                wait(eng, s_const, 0)
                a0.run("gpsimd", eng)
                layer1("gpsimd", eng)


def layout(i):
    a = {n: np.asarray(v) for n, v in i.items()}
    T = lambda x, *axes: np.ascontiguousarray(np.transpose(x, axes) if axes else x.T)
    g = {n[9:]: v for n, v in a.items() if n.startswith("L1_xattn_")}
    cols = np.concatenate([T(g[n].reshape(w, P)) for n, w in COLS], 1)
    heads = lambda w: T(w, 1, 0, 2).reshape(w.shape[1], H * w.shape[2])
    d = dict(x=a["x"], const=CONST, cols=cols, rows=np.stack([g[n] for n in ROWS]),
             ctx=a["ctx_512"], ctxT=T(a["ctx_512"], 0, 2, 1),
             wq0=T(a["L0_xattn_Wq"]), wkv0=T(a["L0_xattn_Wkv"]), wo0=T(a["L0_xattn_Wo"]),
             rw=T(a["L0_ffn_router_w"]), w1e=T(a["L0_ffn_w1"], 0, 2, 1), w2e=T(a["L0_ffn_w2"], 0, 2, 1),
             b1e=a["L0_ffn_b1"], b2e=a["L0_ffn_b2"],
             wg=a["L1_ffn_Wg"], f1=a["L1_ffn_w1"], f2=a["L1_ffn_w2"])
    for p in ("a1", "a2"):
        for n in ("wq", "wk", "wv"):
            d[f"{p}_{n}"] = heads(g[f"{p}_{n}"])
        for n in ("li1", "li2", "li3"):
            d[f"{p}_{n}"] = g[f"{p}_{n}_w"]
    return d


def kernel(**inputs):
    import concourse.bacc as bacc
    from concourse.bass_utils import run_bass_kernel_spmd

    nc = bacc.Bacc("TRN2", target_bir_lowering=False, num_devices=1)
    arrays = {f"in_{n}": np.ascontiguousarray(v) for n, v in layout(inputs).items()}
    t = {n[3:]: nc.dram_tensor(n, v.shape, mybir.dt.from_np(v.dtype), kind="ExternalInput").ap()
         for n, v in arrays.items()}
    for n, rows_ in (("slots_x", SLOTS), ("slots_y", TILES * P)):
        t[n] = nc.dram_tensor(n, (rows_, C), F32, kind="Internal").ap()
    out = nc.dram_tensor("out", (B, S, C), F32, kind="ExternalOutput").ap()
    program(nc, t, out)
    return run_bass_kernel_spmd(nc, [arrays], core_ids=[0]).results[0]["out"]
```
